# Optimizing a Trainium2 kernel written in Bass

```python
import numpy as np
import jax
import jax.numpy as jnp

def _softmax(x, axis=-1):
    return jax.nn.softmax(x, axis=axis)

def _gelu(x):
    return jax.nn.gelu(x, approximate=True)

def _silu(x):
    return jax.nn.silu(x)

def _sigmoid(x):
    return jax.nn.sigmoid(x)

def _layernorm(x, axis=-1, eps=1e-05):
    m = jnp.mean(x, axis=axis, keepdims=True)
    v = jnp.var(x, axis=axis, keepdims=True)
    return (x - m) / jnp.sqrt(v + eps)

def _scatter_add(tgt, idx, src, axis=0):
    return tgt.at[idx].add(src)

def _segment_sum(src, seg, n):
    return jax.ops.segment_sum(src, seg, n)
kernel_name = 'mk_adj_resnorm_d1_adj_r2_a086b0'

def setup_inputs(seed: int=0):
    np.random.seed(seed)
    _w = jnp.asarray

    def _rec_inputs():
        import jax
        import jax.numpy as jnp
        _gk = jax.random.key(seed)
        x = -0.0005963 + 1.001 * jax.random.normal(jax.random.fold_in(_gk, 1), (2048, 256), jnp.float32)
        _a = jax.random.bernoulli(jax.random.fold_in(_gk, 2), 0.00195312, (2048, 2048))
        _a = jnp.logical_or(_a, jnp.swapaxes(_a, -1, -2))
        _a = jnp.logical_or(_a, jnp.eye(2048, dtype=bool))
        _af = _a.astype(jnp.float32)
        adj = _af
        return (x, adj)
    x, adj = _rec_inputs()

    def _L0_gnn_setup():
        import jax, jax.numpy as jnp
        import numpy as np
        N = 3072
        D_IN = 256
        D_OUT = 256
        DENSITY = 0.005
        key = jax.random.key(seed)
        ks = jax.random.split(key, 12)
        x = jax.random.normal(ks[0], (N, D_IN), dtype=jnp.float32)
        adj_a = (jax.random.uniform(ks[1], (N, N)) < DENSITY).astype(jnp.float32)
        adj_b = (jax.random.uniform(ks[2], (N, N)) < DENSITY).astype(jnp.float32)
        W_sa = jax.random.normal(ks[3], (D_IN, D_OUT), dtype=jnp.float32) * (1.414 / np.sqrt(D_IN + D_OUT))
        a_sa = jax.random.normal(ks[4], (1, 2 * D_OUT), dtype=jnp.float32) * (1.414 / np.sqrt(1 + 2 * D_OUT))
        stdv = 1.0 / np.sqrt(D_OUT)
        W_gcnb = jax.random.uniform(ks[5], (D_IN, D_OUT), minval=-stdv, maxval=stdv, dtype=jnp.float32)
        b_gcnb = jax.random.uniform(ks[6], (D_OUT,), minval=-stdv, maxval=stdv, dtype=jnp.float32)
        s = 1.0 / np.sqrt(2 * D_IN)
        Wa = jax.random.uniform(ks[7], (1, 2 * D_IN), minval=-s, maxval=s, dtype=jnp.float32)
        ba = jax.random.uniform(ks[8], (1,), minval=-s, maxval=s, dtype=jnp.float32)
        Wb = jax.random.uniform(ks[9], (1, 2 * D_IN), minval=-s, maxval=s, dtype=jnp.float32)
        bb = jax.random.uniform(ks[10], (1,), minval=-s, maxval=s, dtype=jnp.float32)
        return {'x': x, 'adj_a': adj_a, 'adj_b': adj_b, 'W_sa': W_sa, 'a_sa': a_sa, 'W_gcnb': W_gcnb, 'b_gcnb': b_gcnb, 'Wa': Wa, 'ba': ba, 'Wb': Wb, 'bb': bb}
    _L0_gnn_all = _L0_gnn_setup()
    _L0_gnn_in = {k: v for k, v in _L0_gnn_all.items() if k in ('W_sa', 'a_sa', 'W_gcnb', 'b_gcnb', 'Wa', 'ba', 'Wb', 'bb')}
    del _L0_gnn_all
    return {'x': x, 'adj': adj, 'L0_gnn_W_sa': _L0_gnn_in['W_sa'], 'L0_gnn_a_sa': _L0_gnn_in['a_sa'], 'L0_gnn_W_gcnb': _L0_gnn_in['W_gcnb'], 'L0_gnn_b_gcnb': _L0_gnn_in['b_gcnb'], 'L0_gnn_Wa': _L0_gnn_in['Wa'], 'L0_gnn_ba': _L0_gnn_in['ba'], 'L0_gnn_Wb': _L0_gnn_in['Wb'], 'L0_gnn_bb': _L0_gnn_in['bb']}

def reference(x, adj, L0_gnn_W_sa, L0_gnn_a_sa, L0_gnn_W_gcnb, L0_gnn_b_gcnb, L0_gnn_Wa, L0_gnn_ba, L0_gnn_Wb, L0_gnn_bb):
    import jax
    import jax.numpy as jnp

    def _L0_gnn_ref(x, adj_a, adj_b, W_sa, a_sa, W_gcnb, b_gcnb, Wa, ba, Wb, bb):
        import jax, jax.numpy as jnp
        import numpy as np
        N = 3072
        D_IN = 256
        D_OUT = 256
        DENSITY = 0.005
        type_sum_a = adj_a @ x
        type_sum_b = adj_b @ x
        attn_a = jax.nn.sigmoid(jnp.concatenate([type_sum_a, x], axis=1) @ Wa.T + ba)
        attn_b = jax.nn.sigmoid(jnp.concatenate([type_sum_b, x], axis=1) @ Wb.T + bb)
        h = x @ W_sa
        Hd = h.shape[1]
        s_left = h @ a_sa[0, :Hd]
        s_right = h @ a_sa[0, Hd:]
        scores = s_left[:, None] + s_right[None, :]
        e = jnp.where(adj_a != 0, jnp.exp(-jax.nn.leaky_relu(scores, 0.01)), 0.0)
        attn = e / (jnp.sum(e, axis=1, keepdims=True) + 1e-05)
        x_a = attn @ h
        x_b = adj_b @ (x @ W_gcnb) + b_gcnb
        return jax.nn.sigmoid(attn_a * x_a + attn_b * x_b)
    x = _layernorm(x + _L0_gnn_ref(x, adj, adj, L0_gnn_W_sa, L0_gnn_a_sa, L0_gnn_W_gcnb, L0_gnn_b_gcnb, L0_gnn_Wa, L0_gnn_ba, L0_gnn_Wb, L0_gnn_bb), axis=-1)
    return x

_drawn_inputs = setup_inputs


def setup_inputs(seed=0):
    import zlib

    import numpy as np

    out = dict(_drawn_inputs(seed))
    spreads = {}
    factors = {'L0_gnn_a_sa': 2.97, 'L0_gnn_b_gcnb': 8.0, 'L0_gnn_Wa': 2.918}
    for name, (base, spread) in spreads.items():
        noise = np.random.default_rng([zlib.crc32(name.encode()), seed]).standard_normal(out[name].shape)
        drawn = base * np.exp(spread * noise) if base else spread * noise
        out[name] = jnp.asarray(drawn.astype(out[name].dtype))
    for name, factor in factors.items():
        out[name] = (out[name] * factor).astype(out[name].dtype)
    return out
```

```python
from contextlib import ExitStack

import concourse.bass as bass
from concourse import mybir

P = 128
ALU = mybir.AluOpType
ACT = mybir.ActivationFunctionType
F32 = mybir.dt.float32
F32R = mybir.dt.float32r

SLOPE = 0.01
EPS_ATTN = 1e-5
EPS_NORM = 1e-5


def gnn_layer(nc, x, adj, W_sa, a_sa, W_gcnb, b_gcnb, Wa, ba, Wb, bb, out):
    N, D = x.shape
    TILES = N // P
    KC = D // P
    QB = 4
    QPT = TILES // QB
    QUADS = TILES * QPT
    GT = 2
    QPG = GT * QPT
    GROUPS = TILES // GT
    BODY_TILES = 2 * GT
    BODY = BODY_TILES * QPT
    TURNS = TILES // BODY_TILES
    PRO = 4
    PRO_TURNS = TILES // PRO

    C_LR = D
    C_G = D + 2
    C_NBR = C_G + D
    C_OWN = C_NBR + 2
    WC = C_OWN + 2
    HN = D + 2
    GN = D + 2

    with ExitStack() as ctx:
        def sb(name, shape, dt=F32):
            return ctx.enter_context(nc.sbuf_tensor(name, shape, dt))

        def psum(name):
            return ctx.enter_context(nc.psum_tensor(name, [P, 512], F32))

        def sem(name):
            return ctx.enter_context(nc.semaphore(name))

        ident = sb("ident", [P, P])
        w_raw = sb("w_raw", [P, KC, WC])
        w_hi = sb("w_hi", [P, KC, WC], F32R)
        w_lo = sb("w_lo", [P, KC, WC], F32R)
        gate_rows = sb("gate_rows", [4 * KC, P])
        a_bcast = sb("a_bcast", [P, 2 * D])
        a_prod = sb("a_prod", [P, D])
        bias_row = sb("bias_row", [P, D])
        gate_bias = sb("gate_bias", [P, 2])
        x_in = sb("x_in", [P, 2, 2, D])
        xT_hi = sb("xT_hi", [P, 2, D], F32R)
        xT_lo = sb("xT_lo", [P, 2, D], F32R)
        score_lr = sb("score_lr", [P, TILES, 2])
        own_logit = sb("own_logit", [P, TILES, 2])
        neg_sr = sb("neg_sr", [P, TILES])
        slope_sr = sb("slope_sr", [P, TILES])
        row_scale = sb("row_scale", [P, TILES])
        sl_row = sb("sl_row", [P, N])
        h_hi = sb("h_hi", [P, TILES, HN], F32R)
        h_lo = sb("h_lo", [P, TILES, D], F32R)
        y_hi = sb("y_hi", [P, TILES, GN], F32R)
        y_lo = sb("y_lo", [P, TILES, GN], F32R)
        adj_in = sb("adj_in", [P, 2, N])
        expo = sb("expo", [P, 2, TILES, GT * P])
        adjT = sb("adjT", [P, 4, QB * P], F32R)
        e_full = sb("e_full", [P, 2, QB * P])
        e_hi = sb("e_hi", [P, 4, QB * P], F32R)
        e_lo = sb("e_lo", [P, 4, QB * P], F32R)
        x_res = sb("x_res", [P, 2, D])
        row = sb("row", [P, 2, D])
        gates = sb("gates", [P, 2, 4])
        stats = sb("stats", [P, 2, 6])
        moments = sb("moments", [P, 2, 2])
        rstd = sb("rstd", [P, 2, 1])
        norm_consts = sb("norm_consts", [P, 2])

        tr = [psum(f"tr{i}") for i in range(4)]
        acc_e = [psum(f"acc_e{i}") for i in range(2)]
        acc_g = [psum(f"acc_g{i}") for i in range(2)]

        consts_in = sem("consts_in")
        x_loaded = [sem(f"x_loaded{i}") for i in range(2)]
        adj_loaded = [sem(f"adj_loaded{i}") for i in range(2)]
        xres_loaded = [sem(f"xres_loaded{i}") for i in range(2)]
        stored = [sem(f"stored{i}") for i in range(2)]
        ident_zero = sem("ident_zero")
        ident_ready = sem("ident_ready")
        ones_ready = sem("ones_ready")
        gate_cols_tr = sem("gate_cols_tr")
        gate_cols_ready = sem("gate_cols_ready")
        score_w = sem("score_w")
        w_hi_ready = sem("w_hi_ready")
        w_lo_ready = sem("w_lo_ready")
        xT_tr = sem("xT_tr")
        xT_hi_ready = sem("xT_hi_ready")
        xT_lo_ready = sem("xT_lo_ready")
        proj_done = sem("proj_done")
        h_hi_ready = sem("h_hi_ready")
        y_hi_ready = sem("y_hi_ready")
        proj_used = sem("proj_used")
        sl_tr = sem("sl_tr")
        sl_row_ready = sem("sl_row_ready")
        cols_ready = sem("cols_ready")
        row_scale_ready = sem("row_scale_ready")
        expo_arg = sem("expo_arg")
        expo_ready = sem("expo_ready")
        adj_tr = sem("adj_tr")
        adjT_ready = sem("adjT_ready")
        e_ready = sem("e_ready")
        e_hi_ready = sem("e_hi_ready")
        e_lo_ready = sem("e_lo_ready")
        mm_done = sem("mm_done")
        logit_ready = sem("logit_ready")
        den_ready = sem("den_ready")
        gate_exp = sem("gate_exp")
        gate_sum = sem("gate_sum")
        gate_ready = sem("gate_ready")
        coef_ready = sem("coef_ready")
        g_scaled = sem("g_scaled")
        acc_used = sem("acc_used")
        z_ready = sem("z_ready")
        z_exp = sem("z_exp")
        sig_sum = sem("sig_sum")
        sig_ready = sem("sig_ready")
        y_ready = sem("y_ready")
        stats_ready = sem("stats_ready")
        mom_ready = sem("mom_ready")
        norm_consts_ready = sem("norm_consts_ready")
        var_ready = sem("var_ready")
        rstd_ready = sem("rstd_ready")
        stats_seen = sem("stats_seen")
        rstd_seen = sem("rstd_seen")
        out_ready = sem("out_ready")

        x_pairs = x.rearrange("(n s p) d -> n p s d", s=2, p=P)
        x_rows = x.rearrange("(t p) d -> t p d", p=P)
        adj_rows = adj.rearrange("(t p) j -> t p j", p=P)
        out_rows = out.rearrange("(t p) d -> t p d", p=P)

        LOADED = 16
        CONSTS = 8 * LOADED

        block = ctx.enter_context(nc.Block())

        def exists(it, n):
            return not isinstance(it, int) or BODY * it + n < QUADS

        def run_steps(eng, step):
            for n in range(QPT):
                step(0, n)
            with eng.Fori(0, TURNS - 1) as it:
                for n in range(QPT, QPT + BODY):
                    step(it, n)
            for n in range(QPT, BODY):
                step(TURNS - 1, n)

        @block.sync
        def _(sp):
            nc.sync.dma_start(x_in[:, 0], x_pairs[0]).then_inc(x_loaded[0], 16)
            nc.sync.dma_start(w_raw[:, :, 0:D], W_sa.rearrange("(k p) d -> p k d", p=P)).then_inc(consts_in, 16)
            nc.sync.dma_start(w_raw[:, :, C_G:C_G + D],
                              W_gcnb.rearrange("(k p) d -> p k d", p=P)).then_inc(consts_in, 16)
            nc.sync.dma_start(a_bcast[:], a_sa[0].partition_broadcast(P)).then_inc(consts_in, 16)
            nc.sync.dma_start(gate_rows[0:2 * KC, :],
                              Wa.rearrange("o (c p) -> (o c) p", p=P)).then_inc(consts_in, 16)
            nc.sync.dma_start(gate_rows[2 * KC:4 * KC, :],
                              Wb.rearrange("o (c p) -> (o c) p", p=P)).then_inc(consts_in, 16)
            nc.sync.dma_start(x_in[:, 1], x_pairs[1]).then_inc(x_loaded[1], 16)
            nc.sync.dma_start(bias_row[:], b_gcnb.partition_broadcast(P)).then_inc(consts_in, 16)
            nc.sync.dma_start(gate_bias[:, 0:1], ba.partition_broadcast(P)).then_inc(consts_in, 16)
            nc.sync.dma_start(gate_bias[:, 1:2], bb.partition_broadcast(P)).then_inc(consts_in, 16)
            nc.sync.dma_start(x_res[:, 0], x_rows[0]).then_inc(xres_loaded[0], 16)
            nc.sync.dma_start(x_res[:, 1], x_rows[1]).then_inc(xres_loaded[1], 16)
            with sp.Fori(1, PRO_TURNS) as it:
                for s in range(2):
                    sp.wait_ge(xT_tr, 4 * it + 2 * s - 2)
                    nc.sync.dma_start(x_in[:, s], x_pairs[2 * it + s]).then_inc(x_loaded[s], 16)
            for s in range(2):
                nc.sync.dma_start(adj_in[:, s], adj_rows[s]).then_inc(adj_loaded[s], 16)

            with sp.Fori(0, TILES // 2 - 1) as it:
                for s in range(2):
                    sp.wait_ge(adj_tr, QPT * (2 * it + s) + QPT)
                    nc.sync.dma_start(adj_in[:, s], adj_rows[2 * it + s + 2]).then_inc(adj_loaded[s], 16)
                    sp.wait_ge(out_ready, 2 * it + s + 1)
                    nc.sync.dma_start(out_rows[2 * it + s], row[:, s]).then_inc(stored[s], 16)
                    nc.sync.dma_start(x_res[:, s], x_rows[2 * it + s + 2]).then_inc(xres_loaded[s], 16)
            for s in range(2):
                sp.wait_ge(out_ready, TILES - 1 + s)
                nc.sync.dma_start(out_rows[TILES - 2 + s], row[:, s]).then_inc(stored[s], 16)
            for s in range(2):
                sp.wait_ge(stored[s], LOADED * TILES // 2)

        @block.gpsimd
        def _(pool):
            nc.gpsimd.memset(ident[:], 0.0).then_inc(ident_zero, 1)
            pool.wait_ge(ident_zero, 1)
            nc.gpsimd.affine_select(out=ident[:], in_=ident[:], compare_op=ALU.not_equal, fill=1.0, base=0,
                                    pattern=[[-1, P]], channel_multiplier=1).then_inc(ident_ready, 1)
            nc.gpsimd.memset(h_hi[:, :, D:D + 1].bitcast(F32), 1.0).then_inc(ones_ready, 1)
            nc.gpsimd.memset(h_hi[:, :, D + 1:D + 2].bitcast(F32), 0.0).then_inc(ones_ready, 1)
            nc.gpsimd.memset(norm_consts[:, 0:1], EPS_NORM).then_inc(norm_consts_ready, 1)
            nc.gpsimd.memset(norm_consts[:, 1:2], -0.5).then_inc(norm_consts_ready, 1)
            pool.wait_ge(norm_consts_ready, 2)

            with pool.Fori(0, TILES // 2) as it:
                for slot in range(2):
                    done = 2 * it + slot + 1
                    pool.wait_ge(mom_ready, done)
                    nc.gpsimd.tensor_tensor(rstd[:, slot], moments[:, slot, 1:2], norm_consts[:, 0:1],
                                            ALU.add).then_inc(var_ready, 1)
                    pool.wait_ge(var_ready, done)
                    nc.gpsimd.tensor_tensor(rstd[:, slot], rstd[:, slot], norm_consts[:, 1:2],
                                            ALU.pow).then_inc(rstd_ready, 1)
                    pool.wait_ge(rstd_ready, done)
                    pool.sem_inc(rstd_seen, 1)
                    nc.gpsimd.tensor_scalar(row[:, slot], row[:, slot], moments[:, slot, 0:1], rstd[:, slot],
                                            ALU.subtract, ALU.mult).then_inc(out_ready, 1)

        @block.tensor
        def _(pe):
            pe.wait_ge(ident_ready, 1)
            pe.wait_ge(consts_in, CONSTS)
            nc.tensor.transpose(tr[2][:, 0:4 * KC], gate_rows[:], ident[0:4 * KC, 0:4 * KC]).then_inc(gate_cols_tr, 1)

            def transpose_x(it, s):
                if s % 2 == 0:
                    pe.wait_ge(x_loaded[s // 2 % 2], LOADED * (it + s // PRO) + LOADED)
                if not (isinstance(it, int) and PRO * it + s < 2):
                    pe.wait_ge(xT_lo_ready, PRO * it + s - 1)
                for k in range(KC):
                    last = nc.tensor.transpose(tr[s % 2][:, k * P:(k + 1) * P],
                                               x_in[:, s // 2 % 2, s % 2, k * P:(k + 1) * P], ident[:])
                last.then_inc(xT_tr, 1)

            def project(it, s):
                pe.wait_ge(xT_hi_ready, PRO * it + s + 1)
                pe.wait_ge(xT_lo_ready, PRO * it + s + 1)
                if not (isinstance(it, int) and PRO * it + s < 2):
                    pe.wait_ge(proj_used, PRO * it + s - 1)
                for ps, lo_col, cols in ((acc_e[s % 2], 0, C_G), (acc_g[s % 2], C_G, WC - C_G)):
                    terms = [(xt, w, k) for k in range(KC) for xt, w in ((xT_hi, w_hi), (xT_hi, w_lo), (xT_lo, w_hi))]
                    for n, (xt, w, k) in enumerate(terms):
                        last = nc.tensor.matmul(ps[:, 0:cols], xt[:, s % 2, k * P:(k + 1) * P],
                                                w[:, k, lo_col:lo_col + cols],
                                                start=(n == 0), stop=(n == len(terms) - 1))
                last.then_inc(proj_done, 1)

            transpose_x(0, 0)
            pe.wait_ge(w_hi_ready, 1)
            pe.wait_ge(w_lo_ready, 1)
            transpose_x(0, 1)
            project(0, 0)
            with pe.Fori(0, PRO_TURNS - 1) as it:
                for s in range(1, PRO + 1):
                    transpose_x(it, s + 1)
                    project(it, s)
            for s in range(1, PRO):
                if s + 1 < PRO:
                    transpose_x(PRO_TURNS - 1, s + 1)
                project(PRO_TURNS - 1, s)

            pe.wait_ge(proj_used, TILES)
            for t in range(TILES):
                last = nc.tensor.transpose(tr[t // QB][:, (t % QB) * P:(t % QB + 1) * P],
                                           score_lr[:, t, 0:1].broadcast_to([P, P]), ident[:])
                if t % QB == QB - 1:
                    last.then_inc(sl_tr, 1)

            def transpose_adj(it, n):
                tile, q = n // QPT, n % QPT
                if q == 0:
                    pe.wait_ge(adj_loaded[tile % 2], (LOADED * (BODY_TILES // 2)) * it + LOADED * (tile // 2 + 1))
                if isinstance(it, int) and BODY * it + n < 4:
                    pe.wait_ge(sl_row_ready, n + 1)
                else:
                    pe.wait_ge(adjT_ready, BODY * it + n - 3)
                for b in range(QB):
                    j = (q * QB + b) * P
                    last = nc.tensor.transpose(tr[n % 4][:, b * P:(b + 1) * P], adj_in[:, tile % 2, j:j + P], ident[:])
                last.then_inc(adj_tr, 1)

            def multiply(it, n):
                tile, q = n // QPT, n % QPT
                ps_g, ps_e = acc_g[tile % 2], acc_e[tile % 2]
                if q == 0 and not (isinstance(it, int) and BODY_TILES * it + tile < 2):
                    pe.wait_ge(acc_used, BODY_TILES * it + tile - 1)
                pe.wait_ge(adjT_ready, BODY * it + n + 1)
                pe.wait_ge(e_hi_ready, BODY * it + n + 1)
                for b in range(QB):
                    j = q * QB + b
                    first, end = j == 0, j == TILES - 1
                    blk = adjT[:, n % 4, b * P:(b + 1) * P]
                    nc.tensor.matmul(ps_g[:, 0:GN], blk, y_hi[:, j], start=first, stop=False)
                    nc.tensor.matmul(ps_g[:, 0:GN], blk, y_lo[:, j], start=False, stop=end)
                    blk = e_hi[:, n % 4, b * P:(b + 1) * P]
                    nc.tensor.matmul(ps_e[:, 0:HN], blk, h_hi[:, j], start=first, stop=False)
                    nc.tensor.matmul(ps_e[:, 0:D], blk, h_lo[:, j], start=False, stop=False)
                pe.wait_ge(e_lo_ready, BODY * it + n + 1)
                for b in range(QB):
                    j = q * QB + b
                    last = nc.tensor.matmul(ps_e[:, 0:HN], e_lo[:, n % 4, b * P:(b + 1) * P], h_hi[:, j],
                                            start=False, stop=(j == TILES - 1))
                last.then_inc(mm_done, 1)

            pe.wait_ge(ones_ready, 2)
            for n in range(3):
                transpose_adj(0, n)

            def step(it, n):
                if exists(it, n + 3):
                    transpose_adj(it, n + 3)
                multiply(it, n)

            run_steps(pe, step)

        @block.scalar
        def _(act):
            act.wait_ge(score_w, 2 * KC)
            act.wait_ge(gate_cols_ready, KC)
            nc.scalar.copy(w_hi[:], w_raw[:]).then_inc(w_hi_ready, 1)

            def split_x(it, s):
                act.wait_ge(xT_tr, PRO * it + s + 1)
                if not (isinstance(it, int) and PRO * it + s < 2):
                    act.wait_ge(proj_done, PRO * it + s - 1)
                nc.scalar.copy(xT_hi[:, s % 2], tr[s % 2][:, 0:D]).then_inc(xT_hi_ready, 1)

            def take_projection(it, s):
                t = PRO * it + s
                act.wait_ge(proj_done, PRO * it + s + 1)
                nc.scalar.copy(h_hi[:, bass.ds(t, 1), 0:D], acc_e[s % 2][:, 0:D].unsqueeze(1)).then_inc(h_hi_ready, 1)
                nc.scalar.copy(y_hi[:, bass.ds(t, 1), :], acc_g[s % 2][:, 0:GN].unsqueeze(1)).then_inc(y_hi_ready, 1)

            split_x(0, 0)
            split_x(0, 1)
            take_projection(0, 0)
            with act.Fori(0, PRO_TURNS - 1) as it:
                for s in range(1, PRO + 1):
                    split_x(it, s + 1)
                    take_projection(it, s)
            for s in range(1, PRO):
                if s + 1 < PRO:
                    split_x(PRO_TURNS - 1, s + 1)
                take_projection(PRO_TURNS - 1, s)

            for c in range(TILES // QB):
                act.wait_ge(sl_tr, c + 1)
                nc.scalar.mul(sl_row[:, c * 512:(c + 1) * 512], tr[c][:], SLOPE - 1.0).then_inc(sl_row_ready, 1)
            nc.scalar.activation(row_scale[:], score_lr[:, :, 0], ACT.Exp, scale=-SLOPE).then_inc(row_scale_ready, 1)

            def exponentiate(it, grp, q):
                act.wait_ge(expo_arg, 4 * QPT * it + 2 * (QPT * grp + q) + 2)
                buf = expo[:, grp % 2, QB * q:QB * (q + 1), :]
                nc.scalar.activation(buf, buf, ACT.Exp).then_inc(expo_ready, 1)

            def copy_adjT(it, n):
                act.wait_ge(adj_tr, BODY * it + n + 1)
                if not (isinstance(it, int) and BODY * it + n < 4):
                    act.wait_ge(mm_done, BODY * it + n - 3)
                nc.scalar.copy(adjT[:, n % 4], tr[n % 4][:]).then_inc(adjT_ready, 1)

            def round_e(it, n):
                act.wait_ge(e_ready, BODY * it + n + 1)
                if not (isinstance(it, int) and BODY * it + n < 4):
                    act.wait_ge(mm_done, BODY * it + n - 3)
                nc.scalar.copy(e_hi[:, n % 4], e_full[:, n % 2]).then_inc(e_hi_ready, 1)

            def finish(it, n):
                tile, k = n // QPT - 1, n % QPT
                slot, done = tile % 2, BODY_TILES * it + tile + 1
                if k == 1:
                    act.wait_ge(logit_ready, done)
                    nc.scalar.activation(gates[:, slot, 0:2], gates[:, slot, 0:2], ACT.Exp,
                                         scale=-1.0).then_inc(gate_exp, 1)
                if k == 2:
                    act.wait_ge(gate_ready, done)
                    if not (isinstance(it, int) and BODY_TILES * it + tile < 2):
                        act.wait_ge(stored[slot], (LOADED * BODY_TILES // 2) * it + LOADED * (tile // 2))
                    nc.scalar.mul(row[:, slot], acc_g[slot][:, 0:D], gates[:, slot, 1:2]).then_inc(g_scaled, 1)
                if k == 3:
                    act.wait_ge(z_ready, done)
                    nc.scalar.activation(row[:, slot], row[:, slot], ACT.Exp, scale=-1.0).then_inc(z_exp, 1)

            copy_adjT(0, 0)
            exponentiate(0, 0, 0)
            copy_adjT(0, 1)
            round_e(0, 0)
            for q in range(1, QPT):
                exponentiate(0, 0, q)

            def step(it, n):
                if n >= QPT:
                    finish(it, n)
                if exists(it, n + 2):
                    copy_adjT(it, n + 2)
                if exists(it, n + 1):
                    round_e(it, n + 1)
                if n % 2 == 1 and exists(it, n + QPG):
                    exponentiate(it, n // QPG + 1, n % QPG // 2)

            run_steps(act, step)
            for n in range(BODY, BODY + QPT):
                finish(TURNS - 1, n)

        @block.vector
        def _(dve):
            dve.wait_ge(consts_in, CONSTS)
            for k in range(KC):
                for side in range(2):
                    if k or side:
                        dve.wait_ge(score_w, 2 * k + side)
                    nc.vector.tensor_tensor_reduce(
                        out=a_prod[:], in0=w_raw[:, k, 0:D], in1=a_bcast[:, side * D:(side + 1) * D], scale=1.0,
                        scalar=0.0, op0=ALU.mult, op1=ALU.add,
                        accum_out=w_raw[:, k, C_LR + side:C_LR + side + 1]).then_inc(score_w, 1)
            dve.wait_ge(gate_cols_tr, 1)
            gate_cols = tr[2][:, 0:4 * KC].rearrange("p (b o k) -> p o b k", b=2, o=2)
            for k in range(KC):
                nc.vector.tensor_copy(w_raw[:, k, C_NBR:C_NBR + 4].rearrange("p (o b) -> p o b", o=2),
                                      gate_cols[:, :, :, k]).then_inc(gate_cols_ready, 1)
            dve.wait_ge(w_hi_ready, 1)
            nc.vector.tensor_tensor(w_lo[:], w_raw[:], w_hi[:].bitcast(F32), ALU.subtract).then_inc(w_lo_ready, 1)

            def split_x(it, s):
                dve.wait_ge(xT_hi_ready, PRO * it + s + 1)
                nc.vector.tensor_tensor(xT_lo[:, s % 2], tr[s % 2][:, 0:D], xT_hi[:, s % 2].bitcast(F32),
                                        ALU.subtract).then_inc(xT_lo_ready, 1)

            def take_projection(it, s):
                t = PRO * it + s
                dve.wait_ge(h_hi_ready, PRO * it + s + 1)
                ps_e, ps_g = acc_e[s % 2], acc_g[s % 2]
                nc.vector.tensor_tensor(h_lo[:, bass.ds(t, 1), :], ps_e[:, 0:D].unsqueeze(1),
                                        h_hi[:, bass.ds(t, 1), 0:D].bitcast(F32), ALU.subtract)
                nc.vector.tensor_copy(score_lr[:, bass.ds(t, 1), :], ps_e[:, C_LR:C_LR + 2].unsqueeze(1))
                dve.wait_ge(y_hi_ready, PRO * it + s + 1)
                nc.vector.tensor_tensor(y_lo[:, bass.ds(t, 1), :], ps_g[:, 0:GN].unsqueeze(1),
                                        y_hi[:, bass.ds(t, 1), :].bitcast(F32), ALU.subtract)
                nc.vector.tensor_copy(own_logit[:, bass.ds(t, 1), :],
                                      ps_g[:, GN:GN + 2].unsqueeze(1)).then_inc(proj_used, 1)

            split_x(0, 0)
            split_x(0, 1)
            take_projection(0, 0)
            with dve.Fori(0, PRO_TURNS - 1) as it:
                for s in range(1, PRO + 1):
                    split_x(it, s + 1)
                    take_projection(it, s)
            for s in range(1, PRO):
                if s + 1 < PRO:
                    split_x(PRO_TURNS - 1, s + 1)
                take_projection(PRO_TURNS - 1, s)

            dve.wait_ge(proj_used, TILES)
            nc.vector.tensor_scalar(neg_sr[:], score_lr[:, :, 1], -1.0, None, ALU.mult).then_inc(cols_ready, 1)
            nc.vector.tensor_scalar(slope_sr[:], score_lr[:, :, 1], -SLOPE, None, ALU.mult).then_inc(cols_ready, 1)
            for b in range(2):
                nc.vector.tensor_scalar(own_logit[:, :, b], own_logit[:, :, b], gate_bias[:, b:b + 1], None,
                                        ALU.add).then_inc(cols_ready, 1)
            dve.wait_ge(cols_ready, 4)

            def exponents(it, grp, pair):
                start = (BODY_TILES * P) * it + GT * P * grp
                for j in (2 * pair, 2 * pair + 1):
                    last = nc.vector.tensor_scalar(expo[:, grp % 2, j], sl_row[:, bass.ds(start, GT * P)],
                                                   neg_sr[:, j:j + 1], slope_sr[:, j:j + 1], ALU.add, ALU.min)
                last.then_inc(expo_arg, 1)

            def mask_e(it, n):
                tile, q, grp = n // QPT, n % QPT, n // QPG
                dve.wait_ge(adjT_ready, BODY * it + n + 1)
                dve.wait_ge(expo_ready, 2 * QPT * it + QPT * grp + q + 1)
                if not (isinstance(it, int) and BODY * it + n < 2):
                    dve.wait_ge(e_lo_ready, BODY * it + n - 1)
                nc.vector.scalar_tensor_tensor(
                    out=e_full[:, n % 2].rearrange("p (b i) -> p b i", b=QB),
                    in0=adjT[:, n % 4].bitcast(F32).rearrange("p (b i) -> p b i", b=QB), scalar=0.0,
                    in1=expo[:, grp % 2, q * QB:(q + 1) * QB, (tile % GT) * P:(tile % GT + 1) * P],
                    op0=ALU.not_equal, op1=ALU.mult).then_inc(e_ready, 1)

            def rest_e(it, n):
                dve.wait_ge(e_hi_ready, BODY * it + n + 1)
                nc.vector.tensor_tensor(e_lo[:, n % 4], e_full[:, n % 2], e_hi[:, n % 4].bitcast(F32),
                                        ALU.subtract).then_inc(e_lo_ready, 1)

            def finish(it, n):
                tile, k = n // QPT - 1, n % QPT
                slot, done = tile % 2, BODY_TILES * it + tile + 1
                t = BODY_TILES * it + tile
                gate, r = gates[:, slot], row[:, slot]
                if k == 0:
                    dve.wait_ge(mm_done, BODY * it + n)
                    nc.vector.tensor_tensor(gate[:, 0:2].unsqueeze(1), acc_g[slot][:, D:D + 2].unsqueeze(1),
                                            own_logit[:, bass.ds(t, 1), :], ALU.add).then_inc(logit_ready, 1)
                    if isinstance(it, int) and t == 0:
                        dve.wait_ge(row_scale_ready, 1)
                    nc.vector.tensor_scalar(gate[:, 2:3], acc_e[slot][:, D:D + 1], row_scale[:, bass.ds(t, 1)],
                                            EPS_ATTN, ALU.mult, ALU.add).then_inc(den_ready, 1)
                if k == 1:
                    dve.wait_ge(gate_exp, done)
                    nc.vector.tensor_scalar(gate[:, 0:2], gate[:, 0:2], 1.0, None, ALU.add).then_inc(gate_sum, 1)
                    dve.wait_ge(gate_sum, done)
                    dve.wait_ge(den_ready, done)
                    nc.vector.reciprocal(gate[:, 0:3], gate[:, 0:3]).then_inc(gate_ready, 1)
                    dve.wait_ge(gate_ready, done)
                    nc.vector.tensor_scalar(gate[:, 3:4], gate[:, 2:3], gate[:, 0:1], row_scale[:, bass.ds(t, 1)],
                                            ALU.mult, ALU.mult).then_inc(coef_ready, 1)
                if k == 2:
                    dve.wait_ge(g_scaled, done)
                    dve.wait_ge(coef_ready, done)
                    nc.vector.scalar_tensor_tensor(out=r, in0=acc_e[slot][:, 0:D], scalar=gate[:, 3:4], in1=r,
                                                   op0=ALU.mult, op1=ALU.add).then_inc(acc_used, 1)
                    dve.wait_ge(acc_used, done)
                    nc.vector.scalar_tensor_tensor(out=r, in0=bias_row[:], scalar=gate[:, 1:2], in1=r,
                                                   op0=ALU.mult, op1=ALU.add).then_inc(z_ready, 1)
                if k == 3:
                    dve.wait_ge(z_exp, done)
                    nc.vector.tensor_scalar(r, r, 1.0, None, ALU.add).then_inc(sig_sum, 1)
                    dve.wait_ge(sig_sum, done)
                    nc.vector.reciprocal(r, r).then_inc(sig_ready, 1)
                    dve.wait_ge(sig_ready, done)
                    dve.wait_ge(xres_loaded[slot], (LOADED * BODY_TILES // 2) * it + LOADED * (tile // 2 + 1))
                    nc.vector.tensor_tensor(r, r, x_res[:, slot], ALU.add).then_inc(y_ready, 1)
                    dve.wait_ge(y_ready, done)
                    nc.vector.bn_stats(stats[:, slot], r).then_inc(stats_ready, 1)
                    dve.wait_ge(stats_ready, done)
                    dve.sem_inc(stats_seen, 1)
                    nc.vector.bn_aggr(moments[:, slot], stats[:, slot]).then_inc(mom_ready, 1)

            dve.wait_ge(sl_row_ready, 1)
            for pair in range(2):
                exponents(0, 0, pair)
            mask_e(0, 0)
            for pair in range(2, 2 * QPT):
                exponents(0, 0, pair)
            mask_e(0, 1)
            rest_e(0, 0)

            def step(it, n):
                if exists(it, n + 2):
                    mask_e(it, n + 2)
                if exists(it, n + 1):
                    rest_e(it, n + 1)
                if exists(it, n // QPG * QPG + QPG):
                    if n == 0:
                        dve.wait_ge(sl_row_ready, TILES // QB)
                    dve.wait_ge(e_ready, BODY * it + n + 1)
                    exponents(it, n // QPG + 1, n % QPG)
                if n >= QPT:
                    finish(it, n)

            run_steps(dve, step)
            for n in range(BODY, BODY + QPT):
                finish(TURNS - 1, n)


_INS = ['x', 'adj', 'L0_gnn_W_sa', 'L0_gnn_a_sa', 'L0_gnn_W_gcnb', 'L0_gnn_b_gcnb',
        'L0_gnn_Wa', 'L0_gnn_ba', 'L0_gnn_Wb', 'L0_gnn_bb']
_OUTS = [((2048, 256), 'float32')]


def kernel(**inputs):
    import numpy as _np
    import concourse.bacc as _bacc
    from concourse import mybir as _mybir
    from concourse.bass_utils import run_bass_kernel_spmd as _run

    nc = _bacc.Bacc("TRN2", target_bir_lowering=False, num_devices=1)
    arrays, args = {}, []
    for name in _INS:
        a = _np.ascontiguousarray(inputs[name])
        arrays[f"in_{name}_dram"] = a
        args.append(nc.dram_tensor(f"in_{name}_dram", a.shape, _mybir.dt.from_np(a.dtype), kind="ExternalInput").ap())
    for i, (shape, dtype) in enumerate(_OUTS):
        dt = _mybir.dt.from_np(_np.dtype(dtype))
        args.append(nc.dram_tensor(f"out_{i}_dram", shape, dt, kind="ExternalOutput").ap())
    gnn_layer(nc, *args)
    r = _run(nc, [arrays], core_ids=[0])
    return r.results[0]["out_0_dram"]
```

```python
from contextlib import ExitStack

import concourse.bass as bass
from concourse import mybir

P = 128
ALU = mybir.AluOpType
ACT = mybir.ActivationFunctionType
F32 = mybir.dt.float32
F32R = mybir.dt.float32r

SLOPE = 0.01
EPS_ATTN = 1e-5
EPS_NORM = 1e-5


def gnn_layer(nc, x, adj, W_sa, a_sa, W_gcnb, b_gcnb, Wa, ba, Wb, bb, out):
    N, D = x.shape
    TILES = N // P
    KC = D // P
    QB = 4
    QPT = TILES // QB
    QUADS = TILES * QPT
    GT = 2
    QPG = GT * QPT
    GROUPS = TILES // GT
    BODY_TILES = 2 * GT
    BODY = BODY_TILES * QPT
    TURNS = TILES // BODY_TILES
    LOOK = 4
    PRO = 4
    PRO_TURNS = TILES // PRO
    XR = 2

    C_LR = D
    C_G = D + 2
    C_NBR = C_G + D
    C_OWN = C_NBR + 2
    WC = C_OWN + 2
    HN = D + 2
    GN = D + 2

    with ExitStack() as ctx:
        def sb(name, shape, dt=F32):
            return ctx.enter_context(nc.sbuf_tensor(name, shape, dt))

        def psum(name):
            return ctx.enter_context(nc.psum_tensor(name, [P, 512], F32))

        def sem(name):
            return ctx.enter_context(nc.semaphore(name))

        ident = sb("ident", [P, P])
        ident_r = sb("ident_r", [P, P], F32R)
        w_raw = sb("w_raw", [P, KC, WC])
        w_hi = sb("w_hi", [P, KC, WC], F32R)
        w_lo = sb("w_lo", [P, KC, WC], F32R)
        gate_rows = sb("gate_rows", [4 * KC, P])
        a_bcast = sb("a_bcast", [P, 2 * D])
        a_prod = sb("a_prod", [P, D])
        bias_row = sb("bias_row", [P, D])
        gate_bias = sb("gate_bias", [P, 2])
        x_in = sb("x_in", [P, XR, 2, D])
        xT_hi = sb("xT_hi", [P, PRO, D], F32R)
        xT_lo = sb("xT_lo", [P, PRO, D], F32R)
        score_lr = sb("score_lr", [P, TILES, 2])
        own_logit = sb("own_logit", [P, TILES, 2])
        arg_sr = sb("arg_sr", [P, TILES])
        node_scale = sb("node_scale", [P, TILES, 1])
        row_eps = sb("row_eps", [P, TILES])
        sl_row = sb("sl_row", [P, N])
        h_hi = sb("h_hi", [P, TILES, HN], F32R)
        h_lo = sb("h_lo", [P, TILES, HN], F32R)
        y_hi = sb("y_hi", [P, TILES, GN], F32R)
        y_lo = sb("y_lo", [P, TILES, GN], F32R)
        adj_in = sb("adj_in", [P, 2, N], F32R)
        expo = sb("expo", [P, 2, TILES, GT * P])
        adjT = sb("adjT", [P, 4, QB * P], F32R)
        e_full = sb("e_full", [P, 2, QB * P])
        e_hi = sb("e_hi", [P, 4, QB * P], F32R)
        e_lo = sb("e_lo", [P, 4, QB * P], F32R)
        x_res = sb("x_res", [P, 2, D])
        row = sb("row", [P, 2, D])
        gates = sb("gates", [P, 2, 4])
        stats = sb("stats", [P, 2, 6])
        moments = sb("moments", [P, 2, 2])
        rstd = sb("rstd", [P, 2, 1])
        norm_consts = sb("norm_consts", [P, 2])

        tr = [psum(f"tr{i}") for i in range(4)]
        acc_e = [psum(f"acc_e{i}") for i in range(2)]
        acc_g = [psum(f"acc_g{i}") for i in range(2)]

        consts_in = sem("consts_in")
        biases_in = sem("biases_in")
        x_loaded = [sem(f"x_loaded{i}") for i in range(XR)]
        adj_loaded = [sem(f"adj_loaded{i}") for i in range(2)]
        xres_loaded = [sem(f"xres_loaded{i}") for i in range(2)]
        stored = [sem(f"stored{i}") for i in range(2)]
        ident_zero = sem("ident_zero")
        ident_ready = sem("ident_ready")
        ident_r_ready = sem("ident_r_ready")
        zeros_ready = sem("zeros_ready")
        gate_cols_tr = sem("gate_cols_tr")
        gate_cols_ready = sem("gate_cols_ready")
        score_w = sem("score_w")
        w_hi_ready = sem("w_hi_ready")
        w_lo_ready = sem("w_lo_ready")
        xT_tr = sem("xT_tr")
        xT_hi_ready = sem("xT_hi_ready")
        xT_lo_ready = sem("xT_lo_ready")
        proj_done = sem("proj_done")
        node_scale_ready = sem("node_scale_ready")
        h_hi_ready = sem("h_hi_ready")
        scale_col_hi = sem("scale_col_hi")
        scale_col_lo = sem("scale_col_lo")
        y_hi_ready = sem("y_hi_ready")
        proj_used = sem("proj_used")
        sl_tr = sem("sl_tr")
        sl_row_ready = sem("sl_row_ready")
        cols_ready = sem("cols_ready")
        row_scale_exp = sem("row_scale_exp")
        expo_arg = sem("expo_arg")
        expo_ready = sem("expo_ready")
        adj_tr = sem("adj_tr")
        adjT_ready = sem("adjT_ready")
        e_ready = sem("e_ready")
        e_hi_ready = sem("e_hi_ready")
        e_lo_ready = sem("e_lo_ready")
        mm_done = sem("mm_done")
        logit_ready = sem("logit_ready")
        den_ready = sem("den_ready")
        gate_tanh = sem("gate_tanh")
        den_inv_ready = sem("den_inv_ready")
        gate_ready = sem("gate_ready")
        coef_ready = sem("coef_ready")
        g_scaled = sem("g_scaled")
        acc_used = sem("acc_used")
        z_ready = sem("z_ready")
        z_tanh = sem("z_tanh")
        y_ready = sem("y_ready")
        stats_ready = sem("stats_ready")
        mom_ready = sem("mom_ready")
        norm_consts_ready = sem("norm_consts_ready")
        var_ready = sem("var_ready")
        rstd_ready = sem("rstd_ready")
        stats_seen = sem("stats_seen")
        rstd_seen = sem("rstd_seen")
        out_ready = sem("out_ready")

        x_pairs = x.rearrange("(n s p) d -> n p s d", s=2, p=P)
        x_rows = x.rearrange("(t p) d -> t p d", p=P)
        adj_rows = adj.rearrange("(t p) j -> t p j", p=P)
        out_rows = out.rearrange("(t p) d -> t p d", p=P)

        LOADED = 16
        CONSTS = 5 * LOADED
        BIASES = 3 * LOADED

        sl_banks = [acc_e[0], acc_g[0], acc_e[1], acc_g[1]]

        block = ctx.enter_context(nc.Block())

        def exists(it, n):
            return not isinstance(it, int) or BODY * it + n < QUADS

        def has_node_tile(it, s):
            return not isinstance(it, int) or PRO * it + s < TILES

        def run_node_tiles(eng, node_tile):
            for s in range(2):
                node_tile(0, s)
            with eng.Fori(0, PRO_TURNS - 1) as it:
                for s in range(2, 2 + PRO):
                    node_tile(it, s)
            for s in range(2, PRO):
                node_tile(PRO_TURNS - 1, s)

        def run_steps(eng, step):
            for n in range(QPT):
                step(0, n)
            with eng.Fori(0, TURNS - 1) as it:
                for n in range(QPT, QPT + BODY):
                    step(it, n)
            for n in range(QPT, BODY):
                step(TURNS - 1, n)

        @block.sync
        def _(sp):
            nc.sync.dma_start(w_raw[:, :, 0:D], W_sa.rearrange("(k p) d -> p k d", p=P)).then_inc(consts_in, 16)
            nc.sync.dma_start(a_bcast[:], a_sa[0].partition_broadcast(P)).then_inc(consts_in, 16)
            nc.sync.dma_start(gate_rows[0:2 * KC, :],
                              Wa.rearrange("o (c p) -> (o c) p", p=P)).then_inc(consts_in, 16)
            nc.sync.dma_start(gate_rows[2 * KC:4 * KC, :],
                              Wb.rearrange("o (c p) -> (o c) p", p=P)).then_inc(consts_in, 16)
            nc.sync.dma_start(w_raw[:, :, C_G:C_G + D],
                              W_gcnb.rearrange("(k p) d -> p k d", p=P)).then_inc(consts_in, 16)
            for s in range(XR):
                nc.sync.dma_start(x_in[:, s], x_pairs[s]).then_inc(x_loaded[s], 16)
            with sp.Fori(1, TILES // 2 // XR) as it:
                for s in range(XR):
                    sp.wait_ge(xT_tr, 2 * XR * it + 2 * s + 2 - 2 * XR)
                    nc.sync.dma_start(x_in[:, s], x_pairs[XR * it + s]).then_inc(x_loaded[s], 16)
            nc.sync.dma_start(bias_row[:], b_gcnb.partition_broadcast(P)).then_inc(biases_in, 16)
            nc.sync.dma_start(gate_bias[:, 0:1], ba.partition_broadcast(P)).then_inc(biases_in, 16)
            nc.sync.dma_start(gate_bias[:, 1:2], bb.partition_broadcast(P)).then_inc(biases_in, 16)
            for s in range(2):
                nc.sync.dma_start(x_res[:, s], x_rows[s]).then_inc(xres_loaded[s], 16)
            def store_row(t, s):
                sp.wait_ge(out_ready, t + 1)
                nc.sync.dma_start(out_rows[t], row[:, s]).then_inc(stored[s], 16)

            with sp.Fori(0, TILES // 2 - 1) as it:
                for s in range(2):
                    store_row(2 * it + s, s)
                    nc.sync.dma_start(x_res[:, s], x_rows[2 * it + s + 2]).then_inc(xres_loaded[s], 16)
            for s in range(2):
                store_row(TILES - 2 + s, s)
            for s in range(2):
                sp.wait_ge(stored[s], LOADED * TILES // 2)

        @block.gpsimd
        def _(pool):
            nc.gpsimd.memset(ident[:], 0.0).then_inc(ident_zero, 1)
            pool.wait_ge(ident_zero, 1)
            nc.gpsimd.affine_select(out=ident[:], in_=ident[:], compare_op=ALU.not_equal, fill=1.0, base=0,
                                    pattern=[[-1, P]], channel_multiplier=1).then_inc(ident_ready, 1)
            nc.gpsimd.memset(h_hi[:, :, D + 1:D + 2].bitcast(F32), 0.0).then_inc(zeros_ready, 1)
            nc.gpsimd.memset(h_lo[:, :, D + 1:D + 2].bitcast(F32), 0.0).then_inc(zeros_ready, 1)
            nc.gpsimd.memset(norm_consts[:, 0:1], EPS_NORM).then_inc(norm_consts_ready, 1)
            nc.gpsimd.memset(norm_consts[:, 1:2], -0.5).then_inc(norm_consts_ready, 1)
            pool.wait_ge(norm_consts_ready, 2)

            def load_adj(t, s):
                nc.gpsimd.dma_start(adj_in[:, s], adj_rows[t]).then_inc(adj_loaded[s], 16)

            def reload_adj(t, s):
                pool.wait_ge(adj_tr, QPT * t + QPT)
                load_adj(t + 2, s)

            def normalise(t, slot):
                pool.wait_ge(mom_ready, t + 1)
                nc.gpsimd.tensor_tensor(rstd[:, slot], moments[:, slot, 1:2], norm_consts[:, 0:1],
                                        ALU.add).then_inc(var_ready, 1)
                pool.wait_ge(var_ready, t + 1)
                nc.gpsimd.tensor_tensor(rstd[:, slot], rstd[:, slot], norm_consts[:, 1:2],
                                        ALU.pow).then_inc(rstd_ready, 1)
                pool.wait_ge(rstd_ready, t + 1)
                pool.sem_inc(rstd_seen, 1)
                nc.gpsimd.tensor_scalar(row[:, slot], row[:, slot], moments[:, slot, 0:1], rstd[:, slot],
                                        ALU.subtract, ALU.mult).then_inc(out_ready, 1)

            load_adj(0, 0)
            load_adj(1, 1)
            reload_adj(0, 0)
            with pool.Fori(0, TILES // 2 - 2) as it:
                for s in range(2):
                    reload_adj(2 * it + s + 1, 1 - s)
                    normalise(2 * it + s, s)
            reload_adj(TILES - 3, 1)
            for t in range(TILES - 4, TILES):
                normalise(t, t % 2)

        @block.tensor
        def _(pe):
            pe.wait_ge(ident_ready, 1)
            pe.wait_ge(consts_in, CONSTS)
            nc.tensor.transpose(tr[2][:, 0:4 * KC], gate_rows[:], ident[0:4 * KC, 0:4 * KC]).then_inc(gate_cols_tr, 1)

            def transpose_x(it, s):
                if s % 2 == 0:
                    pe.wait_ge(x_loaded[s // 2 % 2], LOADED * (it + s // PRO) + LOADED)
                if not (isinstance(it, int) and PRO * it + s < PRO):
                    pe.wait_ge(xT_lo_ready, PRO * it + s - PRO + 1)
                for k in range(KC):
                    last = nc.tensor.transpose(tr[s % PRO][:, k * P:(k + 1) * P],
                                               x_in[:, s // 2 % 2, s % 2, k * P:(k + 1) * P], ident[:])
                last.then_inc(xT_tr, 1)

            def project(it, s):
                pe.wait_ge(xT_hi_ready, PRO * it + s + 1)
                pe.wait_ge(xT_lo_ready, PRO * it + s + 1)
                if not (isinstance(it, int) and PRO * it + s < 2):
                    pe.wait_ge(proj_used, PRO * it + s - 1)
                for ps, lo_col, cols in ((acc_e[s % 2], 0, C_G), (acc_g[s % 2], C_G, WC - C_G)):
                    terms = [(xt, w, k) for k in range(KC) for xt, w in ((xT_hi, w_hi), (xT_hi, w_lo), (xT_lo, w_hi))]
                    for n, (xt, w, k) in enumerate(terms):
                        last = nc.tensor.matmul(ps[:, 0:cols], xt[:, s % PRO, k * P:(k + 1) * P],
                                                w[:, k, lo_col:lo_col + cols],
                                                start=(n == 0), stop=(n == len(terms) - 1))
                last.then_inc(proj_done, 1)

            for s in range(2):
                transpose_x(0, s)
            pe.wait_ge(w_hi_ready, 1)
            pe.wait_ge(w_lo_ready, 1)

            def node_tile(it, s):
                if has_node_tile(it, s + 2):
                    transpose_x(it, s + 2)
                project(it, s)

            run_node_tiles(pe, node_tile)

            def spread_sl(c):
                for b in range(QB):
                    last = nc.tensor.transpose(sl_banks[c][:, b * P:(b + 1) * P],
                                               score_lr[:, c * QB + b, 0:1].broadcast_to([P, P]), ident[:])
                last.then_inc(sl_tr, 1)

            pe.wait_ge(proj_used, TILES - 1)
            spread_sl(0)

            def transpose_adj(it, n):
                tile, q = n // QPT, n % QPT
                if q == 0:
                    pe.wait_ge(adj_loaded[tile % 2], (LOADED * (BODY_TILES // 2)) * it + LOADED * (tile // 2 + 1))
                if not (isinstance(it, int) and BODY * it + n < 4):
                    pe.wait_ge(adjT_ready, BODY * it + n - 3)
                for b in range(QB):
                    j = (q * QB + b) * P
                    last = nc.tensor.transpose(tr[n % 4][:, b * P:(b + 1) * P].bitcast(F32R),
                                               adj_in[:, tile % 2, j:j + P], ident_r[:])
                last.then_inc(adj_tr, 1)

            def multiply(it, n):
                tile, q = n // QPT, n % QPT
                ps_g, ps_e = acc_g[tile % 2], acc_e[tile % 2]
                if q == 0 and not (isinstance(it, int) and BODY_TILES * it + tile < 2):
                    pe.wait_ge(acc_used, BODY_TILES * it + tile - 1)
                if q == 0 and isinstance(it, int) and BODY_TILES * it + tile < 2:
                    pe.wait_ge(sl_row_ready, 2 * tile + 2)
                pe.wait_ge(adjT_ready, BODY * it + n + 1)
                pe.wait_ge(e_hi_ready, BODY * it + n + 1)
                for b in range(QB):
                    j = q * QB + b
                    first, end = j == 0, j == TILES - 1
                    blk = adjT[:, n % 4, b * P:(b + 1) * P]
                    nc.tensor.matmul(ps_g[:, 0:GN], blk, y_hi[:, j], start=first, stop=False)
                    nc.tensor.matmul(ps_g[:, 0:GN], blk, y_lo[:, j], start=False, stop=end)
                    blk = e_hi[:, n % 4, b * P:(b + 1) * P]
                    nc.tensor.matmul(ps_e[:, 0:HN], blk, h_hi[:, j], start=first, stop=False)
                    nc.tensor.matmul(ps_e[:, 0:HN], blk, h_lo[:, j], start=False, stop=False)
                pe.wait_ge(e_lo_ready, BODY * it + n + 1)
                for b in range(QB):
                    j = q * QB + b
                    last = nc.tensor.matmul(ps_e[:, 0:HN], e_lo[:, n % 4, b * P:(b + 1) * P], h_hi[:, j],
                                            start=False, stop=(j == TILES - 1))
                last.then_inc(mm_done, 1)

            pe.wait_ge(ident_r_ready, 1)
            for n in range(LOOK):
                transpose_adj(0, n)
            pe.wait_ge(proj_used, TILES)
            for c in range(1, TILES // QB):
                spread_sl(c)
            pe.wait_ge(zeros_ready, 2)
            pe.wait_ge(scale_col_lo, 1)

            def step(it, n):
                if exists(it, n + LOOK):
                    transpose_adj(it, n + LOOK)
                multiply(it, n)

            run_steps(pe, step)

        @block.scalar
        def _(act):
            act.wait_ge(score_w, 2 * KC)
            act.wait_ge(gate_cols_ready, KC)
            nc.scalar.copy(w_hi[:], w_raw[:]).then_inc(w_hi_ready, 1)
            act.wait_ge(ident_ready, 1)
            nc.scalar.copy(ident_r[:], ident[:]).then_inc(ident_r_ready, 1)

            def split_x(it, s):
                act.wait_ge(xT_tr, PRO * it + s + 1)
                if not (isinstance(it, int) and PRO * it + s < PRO):
                    act.wait_ge(proj_done, PRO * it + s - PRO + 1)
                nc.scalar.copy(xT_hi[:, s % PRO], tr[s % PRO][:, 0:D]).then_inc(xT_hi_ready, 1)

            def take_projection(it, s):
                t = PRO * it + s
                act.wait_ge(proj_done, PRO * it + s + 1)
                nc.scalar.activation(node_scale[:, bass.ds(t, 1), :], acc_e[s % 2][:, C_LR + 1:C_LR + 2].unsqueeze(1),
                                     ACT.Exp, scale=-SLOPE).then_inc(node_scale_ready, 1)
                nc.scalar.copy(y_hi[:, bass.ds(t, 1), :], acc_g[s % 2][:, 0:GN].unsqueeze(1)).then_inc(y_hi_ready, 1)
                act.wait_ge(node_scale_ready, PRO * it + s + 1)
                nc.scalar.mul(h_hi[:, bass.ds(t, 1), 0:D], acc_e[s % 2][:, 0:D].unsqueeze(1),
                              node_scale[:, bass.ds(t, 1), 0]).then_inc(h_hi_ready, 1)

            def node_tile(it, s):
                if has_node_tile(it, s + 2):
                    split_x(it, s + 2)
                take_projection(it, s)

            for s in range(2):
                split_x(0, s)
            run_node_tiles(act, node_tile)

            nc.scalar.copy(h_hi[:, :, D], node_scale[:, :, 0]).then_inc(scale_col_hi, 1)

            def take_sl(c):
                act.wait_ge(sl_tr, c + 1)
                nc.scalar.mul(sl_row[:, c * QB * P:(c + 1) * QB * P], sl_banks[c][:],
                              1.0 - SLOPE).then_inc(sl_row_ready, 1)

            def exponentiate(it, grp, q):
                act.wait_ge(expo_arg, 4 * QPT * it + 2 * (QPT * grp + q) + 2)
                buf = expo[:, grp % 2, QB * q:QB * (q + 1), :]
                nc.scalar.activation(buf, buf, ACT.Exp, scale=-1.0).then_inc(expo_ready, 1)

            def copy_adjT(it, n):
                act.wait_ge(adj_tr, BODY * it + n + 1)
                if not (isinstance(it, int) and BODY * it + n < 4):
                    act.wait_ge(mm_done, BODY * it + n - 3)
                nc.scalar.copy(adjT[:, n % 4], tr[n % 4][:]).then_inc(adjT_ready, 1)

            def round_e(it, n):
                act.wait_ge(e_ready, BODY * it + n + 1)
                if not (isinstance(it, int) and BODY * it + n < 4):
                    act.wait_ge(mm_done, BODY * it + n - 3)
                nc.scalar.copy(e_hi[:, n % 4], e_full[:, n % 2]).then_inc(e_hi_ready, 1)

            def finish(it, n):
                tile, k = n // QPT - 1, n % QPT
                slot, done = tile % 2, BODY_TILES * it + tile + 1
                if k == 1:
                    act.wait_ge(logit_ready, done)
                    nc.scalar.activation(gates[:, slot, 0:2], gates[:, slot, 0:2], ACT.Tanh,
                                         scale=0.5).then_inc(gate_tanh, 1)
                if k == 2:
                    act.wait_ge(gate_ready, done)
                    if not (isinstance(it, int) and BODY_TILES * it + tile < 2):
                        act.wait_ge(stored[slot], (LOADED * BODY_TILES // 2) * it + LOADED * (tile // 2))
                    nc.scalar.mul(row[:, slot], acc_g[slot][:, 0:D], gates[:, slot, 1:2]).then_inc(g_scaled, 1)
                if k == 3:
                    act.wait_ge(z_ready, done)
                    nc.scalar.activation(row[:, slot], row[:, slot], ACT.Tanh, scale=0.5).then_inc(z_tanh, 1)

            take_sl(0)
            copy_adjT(0, 0)
            for n in range(1, 3):
                exponentiate(0, 0, n - 1)
                copy_adjT(0, n)
                round_e(0, n - 1)
            for q in range(2, QPT):
                exponentiate(0, 0, q)
            for c in range(1, TILES // QB):
                take_sl(c)
            nc.scalar.activation(row_eps[:], score_lr[:, :, 0], ACT.Exp, scale=SLOPE).then_inc(row_scale_exp, 1)

            def step(it, n):
                if exists(it, n + 3):
                    copy_adjT(it, n + 3)
                if exists(it, n + 2):
                    round_e(it, n + 2)
                if n % 2 == 0 and exists(it, n + QPG):
                    exponentiate(it, n // QPG + 1, n % QPG // 2)
                if n >= QPT:
                    finish(it, n)

            run_steps(act, step)
            for n in range(BODY, BODY + QPT):
                finish(TURNS - 1, n)

        @block.vector
        def _(dve):
            dve.wait_ge(consts_in, CONSTS)
            for k in range(KC):
                for side in range(2):
                    if k or side:
                        dve.wait_ge(score_w, 2 * k + side)
                    nc.vector.tensor_tensor_reduce(
                        out=a_prod[:], in0=w_raw[:, k, 0:D], in1=a_bcast[:, side * D:(side + 1) * D], scale=1.0,
                        scalar=0.0, op0=ALU.mult, op1=ALU.add,
                        accum_out=w_raw[:, k, C_LR + side:C_LR + side + 1]).then_inc(score_w, 1)
            dve.wait_ge(gate_cols_tr, 1)
            gate_cols = tr[2][:, 0:4 * KC].rearrange("p (b o k) -> p o b k", b=2, o=2)
            for k in range(KC):
                nc.vector.tensor_copy(w_raw[:, k, C_NBR:C_NBR + 4].rearrange("p (o b) -> p o b", o=2),
                                      gate_cols[:, :, :, k]).then_inc(gate_cols_ready, 1)
            dve.wait_ge(w_hi_ready, 1)
            nc.vector.tensor_tensor(w_lo[:], w_raw[:], w_hi[:].bitcast(F32), ALU.subtract).then_inc(w_lo_ready, 1)

            def split_x(it, s):
                dve.wait_ge(xT_hi_ready, PRO * it + s + 1)
                nc.vector.tensor_tensor(xT_lo[:, s % PRO], tr[s % PRO][:, 0:D], xT_hi[:, s % PRO].bitcast(F32),
                                        ALU.subtract).then_inc(xT_lo_ready, 1)

            def take_projection(it, s):
                t = PRO * it + s
                ps_e, ps_g = acc_e[s % 2], acc_g[s % 2]
                dve.wait_ge(y_hi_ready, PRO * it + s + 1)
                nc.vector.tensor_tensor(y_lo[:, bass.ds(t, 1), :], ps_g[:, 0:GN].unsqueeze(1),
                                        y_hi[:, bass.ds(t, 1), :].bitcast(F32), ALU.subtract)
                dve.wait_ge(h_hi_ready, PRO * it + s + 1)
                nc.vector.scalar_tensor_tensor(out=h_lo[:, bass.ds(t, 1), 0:D], in0=ps_e[:, 0:D].unsqueeze(1),
                                               scalar=node_scale[:, bass.ds(t, 1), 0],
                                               in1=h_hi[:, bass.ds(t, 1), 0:D].bitcast(F32),
                                               op0=ALU.mult, op1=ALU.subtract)
                nc.vector.tensor_copy(score_lr[:, bass.ds(t, 1), :], ps_e[:, C_LR:C_LR + 2].unsqueeze(1))
                nc.vector.tensor_copy(own_logit[:, bass.ds(t, 1), :],
                                      ps_g[:, GN:GN + 2].unsqueeze(1)).then_inc(proj_used, 1)

            def node_tile(it, s):
                if has_node_tile(it, s + 2):
                    split_x(it, s + 2)
                take_projection(it, s)

            for s in range(2):
                split_x(0, s)
            run_node_tiles(dve, node_tile)

            dve.wait_ge(proj_used, TILES)
            nc.vector.tensor_scalar(arg_sr[:], score_lr[:, :, 1], 1.0 - SLOPE, None, ALU.mult).then_inc(cols_ready, 1)
            dve.wait_ge(scale_col_hi, 1)
            nc.vector.tensor_tensor(h_lo[:, :, D], node_scale[:, :, 0], h_hi[:, :, D].bitcast(F32),
                                    ALU.subtract).then_inc(scale_col_lo, 1)
            dve.wait_ge(cols_ready, 1)

            def exponents(it, grp, pair):
                start = (BODY_TILES * P) * it + GT * P * grp
                for j in (2 * pair, 2 * pair + 1):
                    last = nc.vector.tensor_scalar(expo[:, grp % 2, j], sl_row[:, bass.ds(start, GT * P)],
                                                   arg_sr[:, j:j + 1], 0.0, ALU.add, ALU.max)
                last.then_inc(expo_arg, 1)

            def mask_e(it, n):
                tile, q, grp = n // QPT, n % QPT, n // QPG
                dve.wait_ge(adjT_ready, BODY * it + n + 1)
                dve.wait_ge(expo_ready, 2 * QPT * it + QPT * grp + q + 1)
                if not (isinstance(it, int) and BODY * it + n < 2):
                    dve.wait_ge(e_lo_ready, BODY * it + n - 1)
                nc.vector.scalar_tensor_tensor(
                    out=e_full[:, n % 2].rearrange("p (b i) -> p b i", b=QB),
                    in0=adjT[:, n % 4].bitcast(F32).rearrange("p (b i) -> p b i", b=QB), scalar=0.0,
                    in1=expo[:, grp % 2, q * QB:(q + 1) * QB, (tile % GT) * P:(tile % GT + 1) * P],
                    op0=ALU.not_equal, op1=ALU.mult).then_inc(e_ready, 1)

            def rest_e(it, n):
                dve.wait_ge(e_hi_ready, BODY * it + n + 1)
                nc.vector.tensor_tensor(e_lo[:, n % 4], e_full[:, n % 2], e_hi[:, n % 4].bitcast(F32),
                                        ALU.subtract).then_inc(e_lo_ready, 1)

            def finish(it, n):
                tile, k = n // QPT - 1, n % QPT
                slot, done = tile % 2, BODY_TILES * it + tile + 1
                t = BODY_TILES * it + tile
                gate, r = gates[:, slot], row[:, slot]
                if k == 0:
                    dve.wait_ge(mm_done, BODY * it + n)
                    nc.vector.tensor_tensor(gate[:, 0:2].unsqueeze(1), acc_g[slot][:, D:D + 2].unsqueeze(1),
                                            own_logit[:, bass.ds(t, 1), :], ALU.add).then_inc(logit_ready, 1)
                    nc.vector.tensor_tensor(gate[:, 2:3], acc_e[slot][:, D:D + 1], row_eps[:, bass.ds(t, 1)],
                                            ALU.add).then_inc(den_ready, 1)
                    dve.wait_ge(den_ready, done)
                    nc.vector.reciprocal(gate[:, 2:3], gate[:, 2:3]).then_inc(den_inv_ready, 1)
                if k == 1:
                    dve.wait_ge(gate_tanh, done)
                    nc.vector.tensor_scalar(gate[:, 0:2], gate[:, 0:2], 0.5, 0.5, ALU.mult,
                                            ALU.add).then_inc(gate_ready, 1)
                    dve.wait_ge(gate_ready, done)
                    dve.wait_ge(den_inv_ready, done)
                    nc.vector.tensor_tensor(gate[:, 3:4], gate[:, 2:3], gate[:, 0:1], ALU.mult).then_inc(coef_ready, 1)
                if k == 2:
                    dve.wait_ge(g_scaled, done)
                    dve.wait_ge(coef_ready, done)
                    nc.vector.scalar_tensor_tensor(out=r, in0=acc_e[slot][:, 0:D], scalar=gate[:, 3:4], in1=r,
                                                   op0=ALU.mult, op1=ALU.add).then_inc(acc_used, 1)
                    dve.wait_ge(acc_used, done)
                    nc.vector.scalar_tensor_tensor(out=r, in0=bias_row[:], scalar=gate[:, 1:2], in1=r,
                                                   op0=ALU.mult, op1=ALU.add).then_inc(z_ready, 1)
                if k == 3:
                    dve.wait_ge(z_tanh, done)
                    dve.wait_ge(xres_loaded[slot], (LOADED * BODY_TILES // 2) * it + LOADED * (tile // 2 + 1))
                    nc.vector.scalar_tensor_tensor(out=r, in0=r, scalar=0.5, in1=x_res[:, slot],
                                                   op0=ALU.mult, op1=ALU.add).then_inc(y_ready, 1)
                    dve.wait_ge(y_ready, done)
                    nc.vector.bn_stats(stats[:, slot], r).then_inc(stats_ready, 1)
                    dve.wait_ge(stats_ready, done)
                    dve.sem_inc(stats_seen, 1)
                    nc.vector.bn_aggr(moments[:, slot], stats[:, slot]).then_inc(mom_ready, 1)

            dve.wait_ge(sl_row_ready, 1)
            for pair in range(2):
                exponents(0, 0, pair)
            for n in range(3):
                for pair in (2 * n + 2, 2 * n + 3):
                    exponents(0, 0, pair)
                mask_e(0, n)
                if n:
                    rest_e(0, n - 1)
            for pair in range(2):
                exponents(0, 1, pair)
            dve.wait_ge(biases_in, BIASES)
            for b in range(2):
                nc.vector.tensor_scalar(own_logit[:, :, b], own_logit[:, :, b], gate_bias[:, b:b + 1], None,
                                        ALU.add).then_inc(cols_ready, 1)
            dve.wait_ge(row_scale_exp, 1)
            nc.vector.tensor_scalar(row_eps[:], row_eps[:], EPS_ATTN, None, ALU.mult).then_inc(cols_ready, 1)
            dve.wait_ge(cols_ready, 4)
            dve.wait_ge(sl_row_ready, TILES // QB)

            def step(it, n):
                if exists(it, n + 3):
                    mask_e(it, n + 3)
                if exists(it, n + 2):
                    rest_e(it, n + 2)
                ahead = n + 2
                if exists(it, ahead + QPG):
                    dve.wait_ge(e_ready, BODY * it + n + 2)
                    exponents(it, ahead // QPG + 1, ahead % QPG)
                if n >= QPT:
                    finish(it, n)

            run_steps(dve, step)
            for n in range(BODY, BODY + QPT):
                finish(TURNS - 1, n)


_INS = ['x', 'adj', 'L0_gnn_W_sa', 'L0_gnn_a_sa', 'L0_gnn_W_gcnb', 'L0_gnn_b_gcnb',
        'L0_gnn_Wa', 'L0_gnn_ba', 'L0_gnn_Wb', 'L0_gnn_bb']
_OUTS = [((2048, 256), 'float32')]


def kernel(**inputs):
    import numpy as _np
    import concourse.bacc as _bacc
    from concourse import mybir as _mybir
    from concourse.bass_utils import run_bass_kernel_spmd as _run

    nc = _bacc.Bacc("TRN2", target_bir_lowering=False, num_devices=1)
    arrays, args = {}, []
    for name in _INS:
        a = _np.ascontiguousarray(inputs[name])
        arrays[f"in_{name}_dram"] = a
        args.append(nc.dram_tensor(f"in_{name}_dram", a.shape, _mybir.dt.from_np(a.dtype), kind="ExternalInput").ap())
    for i, (shape, dtype) in enumerate(_OUTS):
        dt = _mybir.dt.from_np(_np.dtype(dtype))
        args.append(nc.dram_tensor(f"out_{i}_dram", shape, dt, kind="ExternalOutput").ap())
    gnn_layer(nc, *args)
    r = _run(nc, [arrays], core_ids=[0])
    return r.results[0]["out_0_dram"]
```

```python
from contextlib import ExitStack

import concourse.bass as bass
from concourse import mybir

P = 128
ALU = mybir.AluOpType
ACT = mybir.ActivationFunctionType
F32 = mybir.dt.float32
F32R = mybir.dt.float32r
BF16 = mybir.dt.bfloat16

SLOPE = 0.01
EPS_ATTN = 1e-5
EPS_NORM = 1e-5


def gnn_layer(nc, x, adj, W_sa, a_sa, W_gcnb, b_gcnb, Wa, ba, Wb, bb, out):
    N, D = x.shape
    TILES = N // P
    KC = D // P
    QB = 4
    QPT = TILES // QB
    QUADS = TILES * QPT
    GT = 2
    QPG = GT * QPT
    GROUPS = TILES // GT
    BODY_TILES = 2 * GT
    BODY = BODY_TILES * QPT
    TURNS = TILES // BODY_TILES
    PRO = 4
    PRO_TURNS = TILES // PRO
    PRO_HEAD = PRO + 2
    FIRST = PRO
    WARM = (9, 8, 1)
    XR = 2

    C_LR = D
    C_G = D + 2
    C_NBR = C_G + D
    C_OWN = C_NBR + 2
    WC = C_OWN + 2
    HN = D + 2
    GN = D + 2

    with ExitStack() as ctx:
        def sb(name, shape, dt=F32):
            return ctx.enter_context(nc.sbuf_tensor(name, shape, dt))

        def psum(name):
            return ctx.enter_context(nc.psum_tensor(name, [P, 512], F32))

        def sem(name):
            return ctx.enter_context(nc.semaphore(name))

        ident = sb("ident", [P, P])
        w_raw = sb("w_raw", [P, KC, WC])
        w_hi = sb("w_hi", [P, KC, WC], F32R)
        w_lo = sb("w_lo", [P, KC, WC], F32R)
        gate_rows = sb("gate_rows", [4 * KC, P])
        a_bcast = sb("a_bcast", [P, 2 * D])
        a_prod = sb("a_prod", [P, 2 * KC, D])
        bias_row = sb("bias_row", [P, D])
        gate_bias = sb("gate_bias", [P, 2])
        x_in = sb("x_in", [P, XR, 2, D])
        xT_hi = sb("xT_hi", [P, PRO, D], F32R)
        xT_lo = sb("xT_lo", [P, PRO, D], F32R)
        score_n99 = sb("score_n99", [P, TILES, 2])
        own_logit = sb("own_logit", [P, TILES, 2])
        node_scale = sb("node_scale", [P, TILES, 1])
        row_eps = sb("row_eps", [P, TILES])
        sl_row = sb("sl_row", [P, N])
        sl_tiles = sb("sl_tiles", [TILES, P])
        sl_dram = nc.dram_tensor("sl_dram", [TILES, P], F32, kind="Internal").ap()
        h_hi = sb("h_hi", [P, TILES, HN], F32R)
        h_lo = sb("h_lo", [P, TILES, HN], F32R)
        y_hi = sb("y_hi", [P, TILES, GN], F32R)
        y_lo = sb("y_lo", [P, TILES, GN], F32R)
        adj_in = sb("adj_in", [P, 2, N], BF16)
        adj_turned = sb("adj_turned", [P, 2, TILES, P], BF16)
        expo = sb("expo", [P, 2, TILES, GT * P])
        adjT = sb("adjT", [P, 4, QB * P], F32R)
        e_full = sb("e_full", [P, 2, QB * P])
        e_hi = sb("e_hi", [P, 4, QB * P], F32R)
        e_lo = sb("e_lo", [P, 4, QB * P], F32R)
        x_res = sb("x_res", [P, 2, D])
        row = sb("row", [P, BODY_TILES, D])
        gates = sb("gates", [P, 2, 4])
        stats = sb("stats", [P, 2, 6])
        moments = sb("moments", [P, 2, 2])
        rstd = sb("rstd", [P, 2, 1])
        norm_consts = sb("norm_consts", [P, 2])

        tr = [psum(f"tr{i}") for i in range(4)]
        acc_e = [psum(f"acc_e{i}") for i in range(2)]
        acc_g = [psum(f"acc_g{i}") for i in range(2)]

        w_sa_in = sem("w_sa_in")
        a_in = sem("a_in")
        w_gcnb_in = sem("w_gcnb_in")
        gate_rows_in = sem("gate_rows_in")
        biases_in = sem("biases_in")
        x_loaded = [sem(f"x_loaded{i}") for i in range(XR)]
        adj_loaded = [sem(f"adj_loaded{i}") for i in range(2)]
        turn_seen = sem("turn_seen")
        turned = [sem(f"turned{i}") for i in range(2)]
        xres_loaded = [sem(f"xres_loaded{i}") for i in range(2)]
        stored = [sem(f"stored{i}") for i in range(BODY_TILES)]
        ident_zero = sem("ident_zero")
        ident_ready = sem("ident_ready")
        zeros_ready = sem("zeros_ready")
        gate_cols_tr = sem("gate_cols_tr")
        score_w = sem("score_w")
        w_sa_hi = sem("w_sa_hi")
        w_sa_lo = sem("w_sa_lo")
        w_gcnb_hi = sem("w_gcnb_hi")
        w_gcnb_lo = sem("w_gcnb_lo")
        small_hi = sem("small_hi")
        score_w_lo = sem("score_w_lo")
        gate_w_lo = sem("gate_w_lo")
        xT_tr = sem("xT_tr")
        xT_hi_ready = sem("xT_hi_ready")
        xT_lo_ready = sem("xT_lo_ready")
        proj_e_done = sem("proj_e_done")
        proj_g_done = sem("proj_g_done")
        node_scale_ready = sem("node_scale_ready")
        h_hi_ready = sem("h_hi_ready")
        h_lo_ready = sem("h_lo_ready")
        scale_col_hi = sem("scale_col_hi")
        scale_col_lo = sem("scale_col_lo")
        y_hi_ready = sem("y_hi_ready")
        y_lo_ready = sem("y_lo_ready")
        sl_tr = sem("sl_tr")
        sl_spread = sem("sl_spread")
        sl_tiles_tr = sem("sl_tiles_tr")
        sl_tiles_ready = sem("sl_tiles_ready")
        sl_in_dram = sem("sl_in_dram")
        sl_loaded = sem("sl_loaded")
        cols_ready = sem("cols_ready")
        row_scale_exp = sem("row_scale_exp")
        expo_ready = sem("expo_ready")
        adjT_ready = [sem(f"adjT_ready{i}") for i in range(2)]
        e_ready = sem("e_ready")
        e_hi_ready = sem("e_hi_ready")
        e_lo_ready = sem("e_lo_ready")
        adj_mm_done = sem("adj_mm_done")
        mm_done = sem("mm_done")
        logit_ready = sem("logit_ready")
        den_ready = sem("den_ready")
        gate_tanh = sem("gate_tanh")
        den_inv_ready = sem("den_inv_ready")
        gate_ready = sem("gate_ready")
        coef_ready = sem("coef_ready")
        g_scaled = sem("g_scaled")
        bias_added = sem("bias_added")
        z_ready = sem("z_ready")
        z_tanh = sem("z_tanh")
        y_ready = sem("y_ready")
        stats_ready = sem("stats_ready")
        mom_ready = sem("mom_ready")
        norm_consts_ready = sem("norm_consts_ready")
        var_ready = sem("var_ready")
        rstd_ready = sem("rstd_ready")
        stats_seen = sem("stats_seen")
        rstd_seen = sem("rstd_seen")
        out_ready = sem("out_ready")

        x_pairs = x.rearrange("(n s p) d -> n p s d", s=2, p=P)
        x_rows = x.rearrange("(t p) d -> t p d", p=P)
        adj_rows = adj.rearrange("(t p) j -> t p j", p=P)
        out_rows = out.rearrange("(t p) d -> t p d", p=P)

        LOADED = 16
        BIASES = 3 * LOADED

        SPREAD = 2
        sl_banks = [tr[2], tr[1]]

        block = ctx.enter_context(nc.Block())

        def exists(it, n):
            return not isinstance(it, int) or BODY * it + n < QUADS

        def run_node_tiles(eng, node_tile):
            for s in range(PRO_HEAD):
                node_tile(0, s)
            with eng.Fori(0, PRO_TURNS - 2) as it:
                for s in range(PRO_HEAD, PRO_HEAD + PRO):
                    node_tile(it, s)

        def run_steps(eng, step, head_step):
            for n in range(QPG):
                head_step(n)
            with eng.Fori(0, TURNS - 1) as it:
                for n in range(QPG, QPG + BODY):
                    step(it, n)
            for n in range(QPG, BODY):
                step(TURNS - 1, n)

        @block.sync
        def _(sp):
            nc.sync.dma_start(x_in[:, 0], x_pairs[0]).then_inc(x_loaded[0], 16)
            nc.sync.dma_start(w_raw[:, :, 0:D], W_sa.rearrange("(k p) d -> p k d", p=P)).then_inc(w_sa_in, 16)
            nc.sync.dma_start(a_bcast[:], a_sa[0].partition_broadcast(P)).then_inc(a_in, 16)
            nc.sync.dma_start(w_raw[:, :, C_G:C_G + D],
                              W_gcnb.rearrange("(k p) d -> p k d", p=P)).then_inc(w_gcnb_in, 16)
            nc.sync.dma_start(gate_rows[0:2 * KC, :],
                              Wa.rearrange("o (c p) -> (o c) p", p=P)).then_inc(gate_rows_in, 16)
            nc.sync.dma_start(gate_rows[2 * KC:4 * KC, :],
                              Wb.rearrange("o (c p) -> (o c) p", p=P)).then_inc(gate_rows_in, 16)
            for s in range(1, XR):
                nc.sync.dma_start(x_in[:, s], x_pairs[s]).then_inc(x_loaded[s], 16)
            with sp.Fori(1, TILES // 2 // XR) as it:
                for s in range(XR):
                    sp.wait_ge(xT_tr, 2 * XR * it + 2 * s + 2 - 2 * XR)
                    nc.sync.dma_start(x_in[:, s], x_pairs[XR * it + s]).then_inc(x_loaded[s], 16)
            for s in range(BODY_TILES):
                sp.sem_inc(stored[s], LOADED)
            nc.sync.dma_start(bias_row[:], b_gcnb.partition_broadcast(P)).then_inc(biases_in, 16)
            nc.sync.dma_start(gate_bias[:, 0:1], ba.partition_broadcast(P)).then_inc(biases_in, 16)
            nc.sync.dma_start(gate_bias[:, 1:2], bb.partition_broadcast(P)).then_inc(biases_in, 16)
            for s in range(2):
                nc.sync.dma_start(x_res[:, s], x_rows[s]).then_inc(xres_loaded[s], 16)
            def turn_adj(it, s):
                sp.wait_ge(adj_loaded[s % 2], LOADED * (BODY_TILES // 2) * it + LOADED * (s // 2 + 1))
                sp.sem_inc(turn_seen, 1)
                if not (isinstance(it, int) and BODY_TILES * it + s < 2):
                    for parity in range(2):
                        sp.wait_ge(adjT_ready[parity], BODY // 2 * it + QPT // 2 * (s - 1))
                        sp.sem_inc(turn_seen, 1)
                nc.sync.dma_start_transpose(adj_turned[:, s % 2], adj_in[:, s % 2]).then_inc(turned[s % 2], 16)

            for s in range(2):
                turn_adj(0, s)
            sp.wait_ge(sl_tiles_ready, 1)
            nc.sync.dma_start(sl_dram, sl_tiles[:]).then_inc(sl_in_dram, 16)
            sp.wait_ge(sl_in_dram, LOADED)
            rest = slice(SPREAD * GT * P, N)
            nc.sync.dma_start(sl_row[:, rest],
                              sl_dram.rearrange("t p -> (t p)")[rest].partition_broadcast(P)).then_inc(sl_loaded, 16)
            for s in range(2, BODY_TILES):
                turn_adj(0, s)

            def store_row(t, s):
                sp.wait_ge(out_ready, t + 1)
                nc.sync.dma_start(out_rows[t], row[:, s]).then_inc(stored[s], 16)

            def load_x_res(t, s):
                nc.sync.dma_start(x_res[:, s % 2], x_rows[t]).then_inc(xres_loaded[s % 2], 16)

            with sp.Fori(0, TURNS - 1) as it:
                for s in range(BODY_TILES):
                    turn_adj(it, s + BODY_TILES)
                    store_row(BODY_TILES * it + s, s)
                    load_x_res(BODY_TILES * it + s + 2, s)
            for s in range(BODY_TILES):
                store_row(TILES - BODY_TILES + s, s)
                if s < BODY_TILES - 2:
                    load_x_res(TILES - BODY_TILES + s + 2, s)
            for s in range(BODY_TILES):
                sp.wait_ge(stored[s], LOADED * (TURNS + 1))

        @block.gpsimd
        def _(pool):
            nc.gpsimd.memset(ident[:], 0.0).then_inc(ident_zero, 1)
            pool.wait_ge(ident_zero, 1)
            nc.gpsimd.affine_select(out=ident[:], in_=ident[:], compare_op=ALU.not_equal, fill=1.0, base=0,
                                    pattern=[[-1, P]], channel_multiplier=1).then_inc(ident_ready, 1)
            nc.gpsimd.memset(h_hi[:, :, D + 1:D + 2].bitcast(F32), 0.0).then_inc(zeros_ready, 1)
            nc.gpsimd.memset(h_lo[:, :, D + 1:D + 2].bitcast(F32), 0.0).then_inc(zeros_ready, 1)
            nc.gpsimd.memset(norm_consts[:, 0:1], EPS_NORM).then_inc(norm_consts_ready, 1)
            nc.gpsimd.memset(norm_consts[:, 1:2], -0.5).then_inc(norm_consts_ready, 1)
            pool.wait_ge(norm_consts_ready, 2)

            def load_adj(it, s):
                t = BODY_TILES * it + s
                if not (isinstance(it, int) and t < 2):
                    pool.wait_ge(turned[s % 2], LOADED * (BODY_TILES // 2) * it + LOADED * (s // 2))
                nc.gpsimd.dma_start(adj_in[:, s % 2], adj_rows[t]).then_inc(adj_loaded[s % 2], 16)

            def deviation(t, slot):
                pool.wait_ge(mom_ready, t + 1)
                nc.gpsimd.tensor_tensor(rstd[:, slot], moments[:, slot, 1:2], norm_consts[:, 0:1],
                                        ALU.add).then_inc(var_ready, 1)
                pool.wait_ge(var_ready, t + 1)
                nc.gpsimd.tensor_tensor(rstd[:, slot], rstd[:, slot], norm_consts[:, 1:2],
                                        ALU.pow).then_inc(rstd_ready, 1)

            def normalise(t, s):
                slot = s % 2
                deviation(t, slot)
                pool.wait_ge(rstd_ready, t + 1)
                pool.sem_inc(rstd_seen, 1)
                nc.gpsimd.tensor_scalar(row[:, s], row[:, s], moments[:, slot, 0:1], rstd[:, slot],
                                        ALU.subtract, ALU.mult).then_inc(out_ready, 1)

            pool.wait_ge(w_sa_hi, 1)
            nc.gpsimd.tensor_tensor(w_lo[:, :, 0:D], w_raw[:, :, 0:D], w_hi[:, :, 0:D].bitcast(F32),
                                    ALU.subtract).then_inc(w_sa_lo, 1)

            pool.wait_ge(x_loaded[0], 2 * LOADED)
            load_adj(0, 0)
            pool.wait_ge(x_loaded[1], 2 * LOADED)
            load_adj(0, 1)
            for s in range(2, BODY_TILES):
                load_adj(0, s)
            with pool.Fori(0, TURNS - 1) as it:
                for s in range(BODY_TILES):
                    load_adj(it, s + BODY_TILES)
                    normalise(BODY_TILES * it + s, s)
            for s in range(BODY_TILES - 1):
                normalise(TILES - BODY_TILES + s, s)
            deviation(TILES - 1, (TILES - 1) % 2)

        @block.tensor
        def _(pe):
            def transpose_x(it, s):
                if s % 2 == 0:
                    pe.wait_ge(x_loaded[s // 2 % 2], LOADED * (it + s // PRO) + LOADED)
                if not (isinstance(it, int) and PRO * it + s < PRO):
                    pe.wait_ge(xT_lo_ready, PRO * it + s - PRO + 1)
                for k in range(KC):
                    last = nc.tensor.transpose(tr[s % PRO][:, k * P:(k + 1) * P],
                                               x_in[:, s // 2 % 2, s % 2, k * P:(k + 1) * P], ident[:])
                last.then_inc(xT_tr, 1)

            def project(it, s):
                pe.wait_ge(xT_hi_ready, PRO * it + s + 1)
                pe.wait_ge(xT_lo_ready, PRO * it + s + 1)
                first_use = isinstance(it, int) and PRO * it + s < 2
                for ps, lo_col, cols, bank_used, done in (
                        (acc_e[s % 2], 0, C_G, h_lo_ready, proj_e_done),
                        (acc_g[s % 2], C_G, WC - C_G, y_lo_ready, proj_g_done)):
                    if not first_use:
                        pe.wait_ge(bank_used, PRO * it + s - 1)
                    if first_use and s == 0 and ps is acc_e[0]:
                        for part in (w_sa_hi, w_sa_lo, score_w_lo):
                            pe.wait_ge(part, 1)
                    if first_use and s == 0 and ps is acc_g[0]:
                        for part in (w_gcnb_hi, w_gcnb_lo, gate_w_lo):
                            pe.wait_ge(part, 1)
                    terms = [(xt, w, k) for k in range(KC) for xt, w in ((xT_hi, w_hi), (xT_hi, w_lo), (xT_lo, w_hi))]
                    for n, (xt, w, k) in enumerate(terms):
                        last = nc.tensor.matmul(ps[:, 0:cols], xt[:, s % PRO, k * P:(k + 1) * P],
                                                w[:, k, lo_col:lo_col + cols],
                                                start=(n == 0), stop=(n == len(terms) - 1))
                    last.then_inc(done, 1)

            def keep_busy(count):
                for _ in range(count):
                    nc.tensor.transpose(acc_g[1][:, 0:P], ident[:], ident[:])

            pe.wait_ge(ident_ready, 1)
            keep_busy(WARM[0])
            transpose_x(0, 0)
            transpose_x(0, 1)
            keep_busy(WARM[1])
            pe.wait_ge(gate_rows_in, 2 * LOADED)
            nc.tensor.transpose(tr[3][:, 0:4 * KC], gate_rows[:], ident[0:4 * KC, 0:4 * KC]).then_inc(gate_cols_tr, 1)

            def spread_sl(grp):
                for k in range(GT):
                    last = nc.tensor.transpose(sl_banks[grp][:, k * P:(k + 1) * P],
                                               score_n99[:, GT * grp + k, 0:1].broadcast_to([P, P]), ident[:])
                last.then_inc(sl_tr, 1)

            def node_tile(it, s):
                if s == FIRST:
                    pe.wait_ge(sl_spread, 1)
                transpose_x(it, s + 2)
                if s == 0:
                    keep_busy(WARM[2])
                if s == FIRST - 1:
                    pe.wait_ge(h_lo_ready, GT)
                    spread_sl(0)
                project(it, s)

            run_node_tiles(pe, node_tile)

            def multiply_adj(it, n):
                tile, q = n // QPT, n % QPT
                ps_g = acc_g[tile % 2]
                if q == 0 and not (isinstance(it, int) and BODY_TILES * it + tile < 2):
                    pe.wait_ge(g_scaled, BODY_TILES * it + tile - 1)
                pe.wait_ge(adjT_ready[n % 2], BODY // 2 * it + n // 2 + 1)
                for b in range(QB):
                    j = q * QB + b
                    blk = adjT[:, n % 4, b * P:(b + 1) * P]
                    nc.tensor.matmul(ps_g[:, 0:GN], blk, y_hi[:, j], start=(j == 0), stop=False)
                    last = nc.tensor.matmul(ps_g[:, 0:GN], blk, y_lo[:, j], start=False, stop=(j == TILES - 1))
                last.then_inc(adj_mm_done, 1)

            def multiply_e(it, n):
                tile, q = n // QPT, n % QPT
                ps_e = acc_e[tile % 2]
                if q == 0 and not (isinstance(it, int) and BODY_TILES * it + tile < 2):
                    pe.wait_ge(z_ready, BODY_TILES * it + tile - 1)
                pe.wait_ge(e_hi_ready, BODY * it + n + 1)
                for b in range(QB):
                    j = q * QB + b
                    blk = e_hi[:, n % 4, b * P:(b + 1) * P]
                    nc.tensor.matmul(ps_e[:, 0:HN], blk, h_hi[:, j], start=(j == 0), stop=False)
                    nc.tensor.matmul(ps_e[:, 0:HN], blk, h_lo[:, j], start=False, stop=False)
                pe.wait_ge(e_lo_ready, BODY * it + n + 1)
                for b in range(QB):
                    j = q * QB + b
                    last = nc.tensor.matmul(ps_e[:, 0:HN], e_lo[:, n % 4, b * P:(b + 1) * P], h_hi[:, j],
                                            start=False, stop=(j == TILES - 1))
                last.then_inc(mm_done, 1)

            project(PRO_TURNS - 1, PRO - 2)
            project(PRO_TURNS - 1, PRO - 1)

            pe.wait_ge(y_lo_ready, TILES - 1)
            multiply_adj(0, 0)
            pe.wait_ge(h_lo_ready, TILES)
            nc.tensor.transpose(tr[0][0:TILES, 0:P], score_n99[:, :, 0], ident[:]).then_inc(sl_tiles_tr, 1)
            spread_sl(1)
            for n in range(1, QPT - 1):
                multiply_adj(0, n)
            pe.wait_ge(y_lo_ready, TILES)
            multiply_adj(0, QPT - 1)
            pe.wait_ge(zeros_ready, 2)
            pe.wait_ge(scale_col_lo, 1)

            def head_step(n):
                if n >= QPT - 1:
                    multiply_adj(0, n + 1)
                multiply_e(0, n)

            def step(it, n):
                if exists(it, n + 1):
                    multiply_adj(it, n + 1)
                multiply_e(it, n)

            run_steps(pe, step, head_step)

        @block.scalar
        def _(act):
            def split_x(it, s):
                act.wait_ge(xT_tr, PRO * it + s + 1)
                if not (isinstance(it, int) and PRO * it + s < PRO):
                    act.wait_ge(proj_g_done, PRO * it + s - PRO + 1)
                nc.scalar.copy(xT_hi[:, s % PRO], tr[s % PRO][:, 0:D]).then_inc(xT_hi_ready, 1)

            def scale_node(it, s):
                t = PRO * it + s
                act.wait_ge(proj_e_done, PRO * it + s + 1)
                nc.scalar.activation(node_scale[:, bass.ds(t, 1), :], acc_e[s % 2][:, C_LR + 1:C_LR + 2].unsqueeze(1),
                                     ACT.Exp, scale=-SLOPE).then_inc(node_scale_ready, 1)

            def take_h(it, s):
                t = PRO * it + s
                act.wait_ge(node_scale_ready, PRO * it + s + 1)
                nc.scalar.mul(h_hi[:, bass.ds(t, 1), 0:D], acc_e[s % 2][:, 0:D].unsqueeze(1),
                              node_scale[:, bass.ds(t, 1), 0]).then_inc(h_hi_ready, 1)

            def take_y(it, s):
                act.wait_ge(proj_g_done, PRO * it + s + 1)
                nc.scalar.copy(y_hi[:, bass.ds(PRO * it + s, 1), :],
                               acc_g[s % 2][:, 0:GN].unsqueeze(1)).then_inc(y_hi_ready, 1)

            def first_exponential(it, j):
                act.wait_ge(h_lo_ready, PRO * it + j + 1)
                nc.scalar.activation(expo[:, 0, bass.ds(PRO * it + j, 1)], sl_row[:, 0:GT * P].unsqueeze(1), ACT.Exp,
                                     bias=score_n99[:, bass.ds(PRO * it + j, 1), 1]).then_inc(expo_ready, 1)

            def node_tile(it, s):
                if s == FIRST - 1:
                    act.wait_ge(sl_tr, 1)
                    nc.scalar.copy(sl_row[:, 0:GT * P], sl_banks[0][:, 0:GT * P]).then_inc(sl_spread, 1)
                if s == FIRST:
                    act.wait_ge(sl_spread, 1)
                scale_node(it, s)
                split_x(it, s + 2)
                take_h(it, s)
                take_y(it, s)
                if s >= FIRST:
                    first_exponential(it, s - FIRST)

            split_x(0, 0)
            act.wait_ge(w_sa_in, LOADED)
            nc.scalar.copy(w_hi[:, :, 0:D], w_raw[:, :, 0:D]).then_inc(w_sa_hi, 1)
            split_x(0, 1)
            act.wait_ge(w_gcnb_in, LOADED)
            nc.scalar.copy(w_hi[:, :, C_G:C_G + D], w_raw[:, :, C_G:C_G + D]).then_inc(w_gcnb_hi, 1)
            run_node_tiles(act, node_tile)

            def exponentiate(it, grp, pair):
                start = (BODY_TILES * P) * it + GT * P * grp
                for j in (2 * pair, 2 * pair + 1):
                    last = nc.scalar.activation(expo[:, grp % 2, j], sl_row[:, bass.ds(start, GT * P)], ACT.Exp,
                                                bias=score_n99[:, j, 1:2])
                last.then_inc(expo_ready, 2)

            def copy_adjT(it, n):
                tile, q = n // QPT, n % QPT
                if q == 0:
                    act.wait_ge(turned[tile % 2], LOADED * (BODY_TILES // 2) * it + LOADED * (tile // 2 + 1))
                if not (isinstance(it, int) and BODY * it + n < 4):
                    act.wait_ge(adj_mm_done, BODY * it + n - 3)
                nc.scalar.copy(adjT[:, n % 4].rearrange("p (b i) -> p b i", b=QB),
                               adj_turned[:, tile % 2, q * QB:(q + 1) * QB]).then_inc(adjT_ready[0], 1)

            def round_e(it, n):
                act.wait_ge(e_ready, BODY * it + n + 1)
                if not (isinstance(it, int) and BODY * it + n < 4):
                    act.wait_ge(mm_done, BODY * it + n - 3)
                nc.scalar.copy(e_hi[:, n % 4], e_full[:, n % 2]).then_inc(e_hi_ready, 1)

            def tanh_gates(it, tile):
                slot = tile % 2
                act.wait_ge(logit_ready, BODY_TILES * it + tile + 1)
                nc.scalar.activation(gates[:, slot, 0:2], gates[:, slot, 0:2], ACT.Tanh,
                                     scale=0.5).then_inc(gate_tanh, 1)

            def scale_g(it, tile):
                slot = tile % 2
                act.wait_ge(gate_ready, BODY_TILES * it + tile + 1)
                act.wait_ge(stored[tile % BODY_TILES], LOADED * it + LOADED * (tile // BODY_TILES + 1))
                nc.scalar.mul(row[:, tile % BODY_TILES], acc_g[slot][:, 0:D], gates[:, slot, 1:2]).then_inc(g_scaled, 1)

            def tanh_z(it, tile):
                act.wait_ge(z_ready, BODY_TILES * it + tile + 1)
                r = row[:, tile % BODY_TILES]
                nc.scalar.activation(r, r, ACT.Tanh, scale=0.5).then_inc(z_tanh, 1)

            copy_adjT(0, 0)
            scale_node(PRO_TURNS - 1, PRO - 2)
            take_h(PRO_TURNS - 1, PRO - 2)
            take_y(PRO_TURNS - 1, PRO - 2)
            scale_node(PRO_TURNS - 1, PRO - 1)
            copy_adjT(0, 2)
            take_h(PRO_TURNS - 1, PRO - 1)
            nc.scalar.copy(h_hi[:, :, D], node_scale[:, :, 0]).then_inc(scale_col_hi, 1)
            take_y(PRO_TURNS - 1, PRO - 1)
            round_e(0, 0)
            for j in range(TILES - 2 - FIRST, TILES - 2):
                first_exponential(0, j)
            round_e(0, 1)
            for j in range(TILES - 2, TILES):
                first_exponential(0, j)
            act.wait_ge(sl_tr, 2)
            nc.scalar.copy(sl_row[:, GT * P:2 * GT * P], sl_banks[1][:, 0:GT * P]).then_inc(sl_spread, 1)
            act.wait_ge(sl_spread, 2)

            def step(it, n):
                if exists(it, n + 3) and n % 2 == 1:
                    copy_adjT(it, n + 3)
                if exists(it, n + 2):
                    round_e(it, n + 2)
                if exists(it, n + QPG):
                    exponentiate(it, n // QPG + 1, n % QPG)
                tile, k = n // QPT, n % QPT
                if k == 0 and tile > 1:
                    tanh_z(it, tile - 2)
                if k == 0 and tile > 0:
                    tanh_gates(it, tile - 1)
                if k == 2 and tile > 0:
                    scale_g(it, tile - 1)

            def head_step(n):
                step(0, n)
                if n == 0:
                    nc.scalar.activation(row_eps[:], score_n99[:, :, 0], ACT.Exp,
                                         scale=-SLOPE / (1.0 - SLOPE)).then_inc(row_scale_exp, 1)
                if n == QPG - 1:
                    act.wait_ge(sl_loaded, LOADED)

            run_steps(act, step, head_step)
            tanh_z(TURNS - 1, BODY_TILES - 2)
            tanh_gates(TURNS - 1, BODY_TILES - 1)
            scale_g(TURNS - 1, BODY_TILES - 1)
            tanh_z(TURNS - 1, BODY_TILES - 1)

        @block.vector
        def _(dve):
            def split_x(it, s):
                dve.wait_ge(xT_hi_ready, PRO * it + s + 1)
                nc.vector.tensor_tensor(xT_lo[:, s % PRO], tr[s % PRO][:, 0:D], xT_hi[:, s % PRO].bitcast(F32),
                                        ALU.subtract).then_inc(xT_lo_ready, 1)

            def take_h(it, s):
                t = PRO * it + s
                dve.wait_ge(h_hi_ready, PRO * it + s + 1)
                nc.vector.tensor_scalar(score_n99[:, bass.ds(t, 1), :], acc_e[s % 2][:, C_LR:C_LR + 2].unsqueeze(1),
                                        SLOPE - 1.0, None, ALU.mult)
                nc.vector.scalar_tensor_tensor(out=h_lo[:, bass.ds(t, 1), 0:D],
                                               in0=acc_e[s % 2][:, 0:D].unsqueeze(1),
                                               scalar=node_scale[:, bass.ds(t, 1), 0],
                                               in1=h_hi[:, bass.ds(t, 1), 0:D].bitcast(F32),
                                               op0=ALU.mult, op1=ALU.subtract).then_inc(h_lo_ready, 1)

            def take_y(it, s):
                t = PRO * it + s
                dve.wait_ge(y_hi_ready, PRO * it + s + 1)
                nc.vector.tensor_copy(own_logit[:, bass.ds(t, 1), :], acc_g[s % 2][:, GN:GN + 2].unsqueeze(1))
                nc.vector.tensor_tensor(y_lo[:, bass.ds(t, 1), :], acc_g[s % 2][:, 0:GN].unsqueeze(1),
                                        y_hi[:, bass.ds(t, 1), :].bitcast(F32), ALU.subtract).then_inc(y_lo_ready, 1)

            def node_tile(it, s):
                split_x(it, s + 2)
                take_h(it, s)
                take_y(it, s)

            split_x(0, 0)
            dve.wait_ge(w_sa_in, LOADED)
            dve.wait_ge(a_in, LOADED)
            for k in range(KC):
                for side in range(2):
                    nc.vector.tensor_tensor_reduce(
                        out=a_prod[:, 2 * k + side], in0=w_raw[:, k, 0:D], in1=a_bcast[:, side * D:(side + 1) * D],
                        scale=1.0, scalar=0.0, op0=ALU.mult, op1=ALU.add,
                        accum_out=w_raw[:, k, C_LR + side:C_LR + side + 1]).then_inc(score_w, 1)
            dve.wait_ge(score_w, 2 * KC)
            nc.vector.tensor_copy(w_hi[:, :, C_LR:C_G], w_raw[:, :, C_LR:C_G]).then_inc(small_hi, 1)
            gate_cols = tr[3][:, 0:4 * KC].rearrange("p (b o k) -> p k o b", b=2, o=2)
            gate_w_hi = w_hi[:, :, C_NBR:C_NBR + 4].rearrange("p k (o b) -> p k o b", o=2)
            dve.wait_ge(gate_cols_tr, 1)
            nc.vector.tensor_copy(gate_w_hi, gate_cols).then_inc(small_hi, 1)
            dve.wait_ge(small_hi, 2)
            nc.vector.tensor_tensor(w_lo[:, :, C_LR:C_G], w_raw[:, :, C_LR:C_G], w_hi[:, :, C_LR:C_G].bitcast(F32),
                                    ALU.subtract).then_inc(score_w_lo, 1)
            nc.vector.tensor_tensor(w_lo[:, :, C_NBR:C_NBR + 4].rearrange("p k (o b) -> p k o b", o=2),
                                    gate_cols, gate_w_hi.bitcast(F32), ALU.subtract).then_inc(gate_w_lo, 1)
            dve.wait_ge(w_gcnb_hi, 1)
            nc.vector.tensor_tensor(w_lo[:, :, C_G:C_G + D], w_raw[:, :, C_G:C_G + D],
                                    w_hi[:, :, C_G:C_G + D].bitcast(F32), ALU.subtract).then_inc(w_gcnb_lo, 1)
            split_x(0, 1)
            run_node_tiles(dve, node_tile)

            def mask_e(it, n):
                tile, q, grp = n // QPT, n % QPT, n // QPG
                dve.wait_ge(adjT_ready[n % 2], BODY // 2 * it + n // 2 + 1)
                dve.wait_ge(expo_ready, GROUPS // TURNS * TILES * it + TILES * grp + QB * q + QB)
                if not (isinstance(it, int) and BODY * it + n < 2):
                    dve.wait_ge(e_lo_ready, BODY * it + n - 1)
                nc.vector.scalar_tensor_tensor(
                    out=e_full[:, n % 2].rearrange("p (b i) -> p b i", b=QB),
                    in0=adjT[:, n % 4].bitcast(F32).rearrange("p (b i) -> p b i", b=QB), scalar=0.0,
                    in1=expo[:, grp % 2, q * QB:(q + 1) * QB, (tile % GT) * P:(tile % GT + 1) * P],
                    op0=ALU.not_equal, op1=ALU.min).then_inc(e_ready, 1)

            def copy_adjT(it, n):
                tile, q = n // QPT, n % QPT
                if q == 1:
                    dve.wait_ge(turned[tile % 2], LOADED * (BODY_TILES // 2) * it + LOADED * (tile // 2 + 1))
                if not (isinstance(it, int) and BODY * it + n < 4):
                    dve.wait_ge(adj_mm_done, BODY * it + n - 3)
                nc.vector.tensor_copy(adjT[:, n % 4].rearrange("p (b i) -> p b i", b=QB),
                                      adj_turned[:, tile % 2, q * QB:(q + 1) * QB]).then_inc(adjT_ready[1], 1)

            def rest_e(it, n):
                dve.wait_ge(e_hi_ready, BODY * it + n + 1)
                nc.vector.tensor_tensor(e_lo[:, n % 4], e_full[:, n % 2], e_hi[:, n % 4].bitcast(F32),
                                        ALU.subtract).then_inc(e_lo_ready, 1)

            def add_logits(it, tile):
                slot = tile % 2
                dve.wait_ge(adj_mm_done, BODY * it + QPT * (tile + 1))
                nc.vector.tensor_tensor(gates[:, slot, 0:2].unsqueeze(1), acc_g[slot][:, D:D + 2].unsqueeze(1),
                                        own_logit[:, bass.ds(BODY_TILES * it + tile, 1), :],
                                        ALU.add).then_inc(logit_ready, 1)

            def make_gates(it, tile):
                gate = gates[:, tile % 2]
                dve.wait_ge(gate_tanh, BODY_TILES * it + tile + 1)
                nc.vector.tensor_scalar(gate[:, 0:2], gate[:, 0:2], 0.5, 0.5, ALU.mult, ALU.add).then_inc(gate_ready, 1)

            def make_coef(it, tile):
                slot, done = tile % 2, BODY_TILES * it + tile + 1
                gate = gates[:, slot]
                dve.wait_ge(mm_done, BODY * it + QPT * (tile + 1))
                nc.vector.tensor_tensor(gate[:, 2:3], acc_e[slot][:, D:D + 1],
                                        row_eps[:, bass.ds(BODY_TILES * it + tile, 1)], ALU.add).then_inc(den_ready, 1)
                dve.wait_ge(den_ready, done)
                nc.vector.reciprocal(gate[:, 2:3], gate[:, 2:3]).then_inc(den_inv_ready, 1)
                dve.wait_ge(den_inv_ready, done)
                dve.wait_ge(gate_ready, done)
                nc.vector.tensor_tensor(gate[:, 3:4], gate[:, 2:3], gate[:, 0:1], ALU.mult).then_inc(coef_ready, 1)

            def add_bias(it, tile):
                slot, done = tile % 2, BODY_TILES * it + tile + 1
                dve.wait_ge(g_scaled, done)
                r = row[:, tile % BODY_TILES]
                nc.vector.scalar_tensor_tensor(out=r, in0=bias_row[:], scalar=gates[:, slot, 1:2], in1=r,
                                               op0=ALU.mult, op1=ALU.add).then_inc(bias_added, 1)

            def add_attention(it, tile):
                slot, done = tile % 2, BODY_TILES * it + tile + 1
                dve.wait_ge(coef_ready, done)
                dve.wait_ge(bias_added, done)
                r = row[:, tile % BODY_TILES]
                nc.vector.scalar_tensor_tensor(out=r, in0=acc_e[slot][:, 0:D], scalar=gates[:, slot, 3:4], in1=r,
                                               op0=ALU.mult, op1=ALU.add).then_inc(z_ready, 1)

            def add_residual(it, tile):
                slot, done = tile % 2, BODY_TILES * it + tile + 1
                r = row[:, tile % BODY_TILES]
                dve.wait_ge(z_tanh, done)
                dve.wait_ge(xres_loaded[slot], (LOADED * BODY_TILES // 2) * it + LOADED * (tile // 2 + 1))
                nc.vector.scalar_tensor_tensor(out=r, in0=r, scalar=0.5, in1=x_res[:, slot],
                                               op0=ALU.mult, op1=ALU.add).then_inc(y_ready, 1)
                dve.wait_ge(y_ready, done)
                nc.vector.bn_stats(stats[:, slot], r).then_inc(stats_ready, 1)
                dve.wait_ge(stats_ready, done)
                dve.sem_inc(stats_seen, 1)
                nc.vector.bn_aggr(moments[:, slot], stats[:, slot]).then_inc(mom_ready, 1)

            copy_adjT(0, 1)
            take_h(PRO_TURNS - 1, PRO - 2)
            take_y(PRO_TURNS - 1, PRO - 2)
            mask_e(0, 0)
            take_h(PRO_TURNS - 1, PRO - 1)
            dve.wait_ge(scale_col_hi, 1)
            nc.vector.tensor_tensor(h_lo[:, :, D], node_scale[:, :, 0], h_hi[:, :, D].bitcast(F32),
                                    ALU.subtract).then_inc(scale_col_lo, 1)
            take_y(PRO_TURNS - 1, PRO - 1)
            copy_adjT(0, 3)
            dve.wait_ge(sl_tiles_tr, 1)
            nc.vector.tensor_copy(sl_tiles[:], tr[0][0:TILES, 0:P]).then_inc(sl_tiles_ready, 1)
            mask_e(0, 1)
            rest_e(0, 0)
            rest_e(0, 1)
            mask_e(0, 2)

            def step(it, n):
                if exists(it, n + 3):
                    mask_e(it, n + 3)
                if exists(it, n + 2):
                    rest_e(it, n + 2)
                if exists(it, n + 4) and n % 2 == 1:
                    copy_adjT(it, n + 4)
                tile, k = n // QPT, n % QPT
                if k == 1 and tile > 0:
                    make_gates(it, tile - 1)
                if k == 1 and tile > 1:
                    add_residual(it, tile - 2)
                if k == 2 and tile > 0:
                    make_coef(it, tile - 1)
                if k == 3 and tile > 0:
                    add_bias(it, tile - 1)
                    add_attention(it, tile - 1)
                if k == 3:
                    add_logits(it, tile)

            def head_step(n):
                if n == 2:
                    dve.wait_ge(y_lo_ready, TILES)
                    dve.wait_ge(biases_in, BIASES)
                    for b in range(2):
                        nc.vector.tensor_scalar(own_logit[:, :, b], own_logit[:, :, b], gate_bias[:, b:b + 1], None,
                                                ALU.add).then_inc(cols_ready, 1)
                    dve.wait_ge(row_scale_exp, 1)
                    nc.vector.tensor_scalar(row_eps[:], row_eps[:], EPS_ATTN, None, ALU.mult).then_inc(cols_ready, 1)
                if n == 3:
                    dve.wait_ge(cols_ready, 3)
                step(0, n)

            run_steps(dve, step, head_step)
            add_residual(TURNS - 1, BODY_TILES - 2)
            last = (TURNS - 1, BODY_TILES - 1)
            make_gates(*last)
            add_bias(*last)
            make_coef(*last)
            add_attention(*last)
            add_residual(*last)
            slot, r = last[1] % 2, row[:, last[1]]
            dve.wait_ge(rstd_ready, TILES)
            nc.vector.tensor_scalar(r, r, moments[:, slot, 0:1], rstd[:, slot],
                                    ALU.subtract, ALU.mult).then_inc(out_ready, 1)


_INS = ['x', 'adj', 'L0_gnn_W_sa', 'L0_gnn_a_sa', 'L0_gnn_W_gcnb', 'L0_gnn_b_gcnb',
        'L0_gnn_Wa', 'L0_gnn_ba', 'L0_gnn_Wb', 'L0_gnn_bb']
_OUTS = [((2048, 256), 'float32')]


def kernel(**inputs):
    import numpy as _np
    import concourse.bacc as _bacc
    from concourse import mybir as _mybir
    from concourse.bass_utils import run_bass_kernel_spmd as _run

    nc = _bacc.Bacc("TRN2", target_bir_lowering=False, num_devices=1)
    arrays, args = {}, []
    for name in _INS:
        a = _np.ascontiguousarray(inputs[name])
        arrays[f"in_{name}_dram"] = a
        args.append(nc.dram_tensor(f"in_{name}_dram", a.shape, _mybir.dt.from_np(a.dtype), kind="ExternalInput").ap())
    for i, (shape, dtype) in enumerate(_OUTS):
        dt = _mybir.dt.from_np(_np.dtype(dtype))
        args.append(nc.dram_tensor(f"out_{i}_dram", shape, dt, kind="ExternalOutput").ap())
    gnn_layer(nc, *args)
    r = _run(nc, [arrays], core_ids=[0])
    return r.results[0]["out_0_dram"]
```
